# Optimizing a Trainium2 kernel written in Bass

```python
import numpy as np
import jax
import jax.numpy as jnp

def _softmax(x, axis=-1):
    return jax.nn.softmax(x, axis=axis)

def _gelu(x):
    return jax.nn.gelu(x, approximate=True)

def _silu(x):
    return jax.nn.silu(x)

def _sigmoid(x):
    return jax.nn.sigmoid(x)

def _layernorm(x, axis=-1, eps=1e-05):
    m = jnp.mean(x, axis=axis, keepdims=True)
    v = jnp.var(x, axis=axis, keepdims=True)
    return (x - m) / jnp.sqrt(v + eps)

def _scatter_add(tgt, idx, src, axis=0):
    return tgt.at[idx].add(src)

def _segment_sum(src, seg, n):
    return jax.ops.segment_sum(src, seg, n)
kernel_name = 'mk_adj_ffn_d1_adj_r2_a7053f'

def setup_inputs(seed: int=0):
    np.random.seed(seed)
    _w = jnp.asarray

    def _rec_inputs():
        import jax
        import jax.numpy as jnp
        _gk = jax.random.key(seed)
        x = -0.0005207 + 1.001 * jax.random.normal(jax.random.fold_in(_gk, 1), (16, 512, 128), jnp.float32)
        _a = jax.random.bernoulli(jax.random.fold_in(_gk, 2), 0.0078125, (16, 512, 512))
        adj = _a.astype(jnp.int32)
        return (x, adj)
    x, adj = _rec_inputs()

    def _L0_gnn_setup():
        import jax, jax.numpy as jnp
        import numpy as np
        B, N, F_IN, F_OUT = (1, 4096, 128, 128)
        ALPHA = 0.2
        NEG_INF = -9000000000000000.0
        key = jax.random.key(seed)
        ks = jax.random.split(key, 8)
        feat = jax.random.normal(ks[0], (B, N, F_IN), dtype=jnp.float32)
        adj = jax.random.randint(ks[1], (B, N, N), 0, 2, dtype=jnp.int32)
        s = 1.414 * (6.0 / (F_IN + F_OUT)) ** 0.5
        W = jax.random.uniform(ks[2], (F_IN, F_OUT), minval=-s, maxval=s, dtype=jnp.float32)
        a_1 = jax.random.normal(ks[3], (F_OUT, 1), dtype=jnp.float32) * 0.1
        a_2 = jax.random.normal(ks[4], (F_OUT, 1), dtype=jnp.float32) * 0.1
        a_12 = jax.random.normal(ks[5], (F_OUT, F_OUT), dtype=jnp.float32) * (1.0 / F_OUT ** 0.5)
        W_1 = jax.random.uniform(ks[6], (F_IN, F_OUT), minval=-s, maxval=s, dtype=jnp.float32)
        W_2 = jax.random.uniform(ks[7], (F_IN, F_OUT), minval=-s, maxval=s, dtype=jnp.float32)
        return {'feat': feat, 'adj': adj, 'W': W, 'a_1': a_1, 'a_2': a_2, 'a_12': a_12, 'W_1': W_1, 'W_2': W_2}
    _L0_gnn_all = _L0_gnn_setup()
    _L0_gnn_in = {k: v for k, v in _L0_gnn_all.items() if k in ('W', 'a_1', 'a_2', 'a_12', 'W_1', 'W_2')}
    del _L0_gnn_all

    def _L0_ffn_setup():
        import jax, jax.numpy as jnp
        import numpy as np
        B, S, H, F, E, K = (8, 2048, 128, 256, 16, 2)
        EPS = 1e-05
        key = jax.random.key(seed)
        ks = jax.random.split(key, 9)
        sc = 0.02
        return {'x': jax.random.normal(ks[0], (B, S, H), dtype=jnp.float32), 'gate_w': jax.random.normal(ks[1], (H, E), dtype=jnp.float32) * sc, 'gate_b': jnp.zeros((E,), dtype=jnp.float32), 'w1': jax.random.normal(ks[2], (E, H, F), dtype=jnp.float32) * sc, 'b1': jnp.zeros((E, F), dtype=jnp.float32), 'w2': jax.random.normal(ks[3], (E, F, H), dtype=jnp.float32) * sc, 'b2': jnp.zeros((E, H), dtype=jnp.float32), 'gamma': jnp.ones((H,), dtype=jnp.float32), 'beta': jnp.zeros((H,), dtype=jnp.float32)}
    _L0_ffn_all = _L0_ffn_setup()
    _L0_ffn_in = {k: v for k, v in _L0_ffn_all.items() if k in ('gate_w', 'gate_b', 'w1', 'b1', 'w2', 'b2', 'gamma', 'beta')}
    del _L0_ffn_all
    return {'x': x, 'adj': adj, 'L0_gnn_W': _L0_gnn_in['W'], 'L0_gnn_a_1': _L0_gnn_in['a_1'], 'L0_gnn_a_2': _L0_gnn_in['a_2'], 'L0_gnn_a_12': _L0_gnn_in['a_12'], 'L0_gnn_W_1': _L0_gnn_in['W_1'], 'L0_gnn_W_2': _L0_gnn_in['W_2'], 'L0_ffn_gate_w': _L0_ffn_in['gate_w'], 'L0_ffn_gate_b': _L0_ffn_in['gate_b'], 'L0_ffn_w1': _L0_ffn_in['w1'], 'L0_ffn_b1': _L0_ffn_in['b1'], 'L0_ffn_w2': _L0_ffn_in['w2'], 'L0_ffn_b2': _L0_ffn_in['b2'], 'L0_ffn_gamma': _L0_ffn_in['gamma'], 'L0_ffn_beta': _L0_ffn_in['beta']}

def reference(x, adj, L0_gnn_W, L0_gnn_a_1, L0_gnn_a_2, L0_gnn_a_12, L0_gnn_W_1, L0_gnn_W_2, L0_ffn_gate_w, L0_ffn_gate_b, L0_ffn_w1, L0_ffn_b1, L0_ffn_w2, L0_ffn_b2, L0_ffn_gamma, L0_ffn_beta):
    import jax
    import jax.numpy as jnp

    def _L0_gnn_ref(feat, adj, W, a_1, a_2, a_12, W_1, W_2):
        import jax, jax.numpy as jnp
        import numpy as np
        B, N, F_IN, F_OUT = (1, 4096, 128, 128)
        ALPHA = 0.2
        NEG_INF = -9000000000000000.0
        h = jnp.matmul(feat, W)
        Ax = jnp.matmul(h, a_1)
        Ay = jnp.matmul(h, a_2)
        A_xy = jnp.matmul(jnp.matmul(h, a_12), jnp.swapaxes(h, 1, 2))
        logits = jnp.swapaxes(Ax, 1, 2) + Ay + A_xy
        e = jax.nn.leaky_relu(logits, negative_slope=ALPHA)
        e = jnp.where(adj > 0, e, NEG_INF)
        attention = jax.nn.softmax(e, axis=-1)
        h_prime = jnp.matmul(attention, feat)
        h_out = jnp.matmul(feat, W_1) + jnp.matmul(h_prime, W_2)
        return jax.nn.elu(h_out)

    def _L0_ffn_ref(x, gate_w, gate_b, w1, b1, w2, b2, gamma, beta):
        import jax, jax.numpy as jnp
        import numpy as np
        B, S, H, F, E, K = (8, 2048, 128, 256, 16, 2)
        EPS = 1e-05
        gate_logits = x @ gate_w + gate_b
        topk_vals, topk_idx = jax.lax.top_k(gate_logits, K)
        topk_w = jax.nn.softmax(topk_vals, axis=-1)
        h = jax.nn.relu(jnp.einsum('bsh,ehf->bsef', x, w1) + b1)
        expert_out = jnp.einsum('bsef,efh->bseh', h, w2) + b2
        sel = jnp.take_along_axis(expert_out, topk_idx[:, :, :, None], axis=2)
        moe = jnp.sum(topk_w[..., None] * sel, axis=2)
        y = x + moe
        mu = jnp.mean(y, axis=-1, keepdims=True)
        var = jnp.var(y, axis=-1, keepdims=True)
        return (y - mu) / jnp.sqrt(var + EPS) * gamma + beta
    x = x + _L0_gnn_ref(_layernorm(x, axis=-1), adj, L0_gnn_W, L0_gnn_a_1, L0_gnn_a_2, L0_gnn_a_12, L0_gnn_W_1, L0_gnn_W_2)
    x = x + _L0_ffn_ref(_layernorm(x, axis=-1), L0_ffn_gate_w, L0_ffn_gate_b, L0_ffn_w1, L0_ffn_b1, L0_ffn_w2, L0_ffn_b2, L0_ffn_gamma, L0_ffn_beta)
    return x

_drawn_inputs = setup_inputs


def setup_inputs(seed=0):
    import zlib

    import numpy as np

    out = dict(_drawn_inputs(seed))
    spreads = {'L0_ffn_gate_b': (0.0, 0.334),
     'L0_ffn_b1': (0.0, 0.8),
     'L0_ffn_b2': (0.0, 0.308),
     'L0_ffn_gamma': (1.0, 0.2),
     'L0_ffn_beta': (0.0, 0.1)}
    factors = {'L0_gnn_a_2': 5.115, 'L0_ffn_w1': 4.955, 'L0_ffn_w2': 3.901}
    for name, (base, spread) in spreads.items():
        noise = np.random.default_rng([zlib.crc32(name.encode()), seed]).standard_normal(out[name].shape)
        drawn = base * np.exp(spread * noise) if base else spread * noise
        out[name] = jnp.asarray(drawn.astype(out[name].dtype))
    for name, factor in factors.items():
        out[name] = (out[name] * factor).astype(out[name].dtype)
    return out
```

```python
from contextlib import ExitStack

import concourse.bass as bass
from concourse import mybir

F32 = mybir.dt.float32
BF16 = mybir.dt.bfloat16
I32 = mybir.dt.int32
U32 = mybir.dt.uint32
ALU = mybir.AluOpType
ACT = mybir.ActivationFunctionType
AX_X = mybir.AxisListType.X

P = 128
ALPHA = 0.2
NEG_INF = -9e15
EPS = 1e-5
FAR = float(1 << 20)


def graph_attention_and_routed_experts(nc, x, adj, W, a_1, a_2, a_12, W_1, W_2, gate_w, gate_b, w1, b1, w2, b2,
                                       gamma, beta, out):
    G, N, D = x.shape
    TPG = N // P
    TILES = G * TPG
    TOK = G * N
    E, _, F = w1.shape
    FC = F // P
    K = 2
    assert D == P and N == 512 and FC == 2 and E == 16

    META = 2
    ROW = D + META
    BIN = TOK + P
    PAD_ROW = E * BIN
    TU = 4
    XT = TOK * K // P + E
    assert XT % TU == 0
    TURNS = XT // TU

    bins = nc.dram_tensor("expert_bins", (PAD_ROW + P, ROW), F32, kind="Internal").ap()
    results = nc.dram_tensor("expert_results", (TOK * K, D), F32, kind="Internal").ap()

    with ExitStack() as ctx:
        def sb(name, shape, dt=F32):
            return ctx.enter_context(nc.sbuf_tensor(name, shape, dt))

        def sem(name):
            return ctx.enter_context(nc.semaphore(name))

        bank = [ctx.enter_context(nc.psum_tensor(f"bank{i}", [P, 512], F32)) for i in range(8)]

        ident = sb("ident", [P, P])
        ident_bf = sb("ident_bf", [P, P], BF16)
        ones_bf = sb("ones_bf", [P, P], BF16)
        before_bf = sb("before_bf", [P, P], BF16)
        expert_no = sb("expert_no", [P, E])
        bin_start = sb("bin_start", [P, E])
        tile_no = sb("tile_no", [P, XT])
        half = sb("half", [P, 2 * TPG])
        pad_rows = sb("pad_rows", [P, ROW])
        W_sb = sb("W_sb", [P, D])
        a12_sb = sb("a12_sb", [P, D])
        a1_sb = sb("a1_sb", [P, 1])
        a2_sb = sb("a2_sb", [P, 1])
        WT = sb("WT", [P, D])
        a12T = sb("a12T", [P, D])
        C_sb = sb("C_sb", [P, D])
        M_sb = sb("M_sb", [P, D])
        u1 = sb("u1", [P, 1])
        u2 = sb("u2", [P, 1])
        W21 = sb("W21", [P, 2 * D])
        gate_sb = sb("gate_sb", [P, E])
        gate_bias = sb("gate_bias", [P, E])
        w1_sb = sb("w1_sb", [P, E * F])
        w2_sb = sb("w2_sb", [P, E * FC * D])
        b1_rows = sb("b1_rows", [E * FC, P])
        b1_cols = sb("b1_cols", [P, E * FC])
        b2_all = sb("b2_all", [P, E * D])
        gamma_all = sb("gamma_all", [P, D])
        beta_all = sb("beta_all", [P, D])

        x_sb = sb("x_sb", [P, TILES, D])
        xn_all = sb("xn_all", [P, TILES, D])
        token2 = sb("token2", [P, TILES])
        ay4 = sb("ay4", [P, TILES])
        row_min = sb("row_min", [P, TPG])
        row_sum = sb("row_sum", [P, TILES])
        gap = sb("gap", [P, TILES])

        adj_sb = sb("adj_sb", [P, TPG, N], I32)
        no_edge = sb("no_edge", [P, TPG, N], BF16)
        feat = sb("feat", [P, TPG, D])
        featT = sb("featT", [P, N])
        qT = sb("qT", [P, N])
        vh = sb("vh", [P, TPG, 2 * D])
        relu4 = sb("relu4", [P, 2, N])
        prob = sb("prob", [P, TPG, N])
        probT = sb("probT", [P, 2, N])
        z = sb("z", [P, TPG, D])
        zneg = sb("zneg", [P, TPG, D])
        rinv = sb("rinv", [P, TPG])
        bn = sb("bn", [P, 2 * TPG, 6])
        mv = sb("mv", [P, 2 * TPG, 2])
        var_eps = sb("var_eps", [P, 2 * TPG])
        rstd = sb("rstd", [P, 2 * TPG])
        row = sb("row", [P, TPG, ROW])
        row_out = sb("row_out", [P, TPG, ROW])
        slots = sb("slots", [P, TPG, K], U32)
        x2T = sb("x2T", [P, N])
        logit = sb("logit", [P, TPG, E])
        top = sb("top", [P, TPG, 8])
        top_no = sb("top_no", [P, TPG, 8], U32)
        chosen = sb("chosen", [P, TPG, K])
        onehot = sb("onehot", [P, TPG * K, E])
        member = sb("member", [P, TPG, E], BF16)
        base = sb("base", [P, E])
        place = sb("place", [P, TPG, E])
        picked = sb("picked", [P, TPG * K, E])

        base_i = sb("base_i", [P, E], I32)
        cnt = sb("cnt", [P, E])
        cnt_i = sb("cnt_i", [P, E], I32)
        ntile_i = sb("ntile_i", [P, E], I32)
        PADC = 8
        scan = [sb(f"scan{i}", [P, PADC + E]) for i in range(2)]
        passed = sb("passed", [P, XT, E])
        expert_of = sb("expert_of", [P, XT])
        start_of = sb("start_of", [P, XT])
        first_row = sb("first_row", [P, XT])
        first_row_i = sb("first_row_i", [P, XT], I32)
        expert_w = sb("expert_w", [P, XT])
        expert_i = sb("expert_i", [P, XT + 1], I32)

        xg = sb("xg", [P, TU, ROW])
        xgT = sb("xgT", [P, 2, P])
        hid = sb("hid", [P, 2, F])
        hidT = sb("hidT", [P, 2, F])
        y = sb("y", [P, TU, D])
        dest = sb("dest", [P, TU], U32)

        wexp = sb("wexp", [P, TILES])
        wsum = sb("wsum", [P, TILES])
        wt = sb("wt", [P, K, TILES])
        yy = sb("yy", [P, 2, TPG, K * D])
        acc = sb("acc", [P, TPG, D])
        outn = sb("outn", [P, 2, TPG, D])

        s_early, s_gnn_w, s_late, s_const = sem("early_loaded"), sem("gnn_weights_loaded"), sem("late_loaded"), sem("constants_made")
        s_wt, s_wt_sb = sem("setup_matmul_done"), sem("setup_copied")
        s_x, s_adj = sem("x_loaded"), sem("adj_loaded")
        s_mask = sem("mask_made")
        s_bn, s_bn1, s_bn2 = sem("first_stats_made"), sem("feat_stats_made"), sem("row_stats_made")
        s_mv1, s_mv2, s_rs = sem("feat_variances_made"), sem("row_variances_made"), sem("rstd_made")
        s_row_out, s_row_kept, s_slots = sem("row_out_copied"), sem("row_kept"), sem("slot_steps")
        s_pow = sem("rstd_step")
        s_feat, s_x2n = sem("feat_made"), sem("rows_made")
        s_ft, s_ft_sb = sem("featT_done"), sem("featT_copied")
        s_qt, s_qt_sb = sem("qT_done"), sem("qT_copied")
        s_small, s_ay = sem("ay_and_logits_done"), sem("ay_copied")
        s_hv, s_hv_sb = sem("vh_done"), sem("vh_copied")
        s_s, s_relu, s_em, s_exp = sem("scores_done"), sem("relu_made"), sem("masked_logits_made"), sem("prob_made")
        s_pt, s_pta, s_ptd = sem("probT_done"), sem("probT_even_copied"), sem("probT_odd_copied")
        s_pv, s_z, s_zneg, s_e = sem("pv_done"), sem("z_made"), sem("zneg_made"), sem("elu_exp_made")
        s_zs = sem("z_steps")
        s_x2t, s_x2t_sb = sem("x2T_done"), sem("x2T_copied")
        s_gate = sem("gate_steps")
        s_member, s_rank, s_slot = sem("member_made"), sem("rank_done"), sem("slots_made")
        s_bin = sem("rows_in_bins")
        s_tab, s_tab_done, s_pad = sem("table_steps"), sem("table_made"), sem("padding_written")
        s_padrow = sem("pad_tile_written")
        s_xg = [sem(f"tokens_loaded_{u}") for u in range(TU)]
        s_tx, s_xgt = sem("xgT_done"), sem("xgT_copied")
        s_mm1, s_h, s_ht, s_hr = sem("hidden_done"), sem("hidden_copied"), sem("hiddenT_done"), sem("hidden_relu_made")
        s_mm2, s_y = sem("expert_out_done"), sem("expert_out_made")
        s_sc = [sem(f"results_scattered_{u}") for u in range(TU)]
        s_gap, s_w = sem("gate_exp_made"), sem("weight_steps")
        s_yy = [sem(f"results_loaded_{u}") for u in range(2)]
        s_fin, s_fmv, s_frs, s_fn, s_fo = sem("final_steps"), sem("final_var"), sem("final_rstd"), sem("final_scaled"), sem("final_made")
        s_out = [sem(f"out_stored_{u}") for u in range(2)]

        s_settled = {name: sem(f"waited_{name}") for name in ("Pool", "DVE")}

        def wait_for(eng, s, value):
            if not isinstance(value, int) or value > 0:
                eng.wait_ge(s, value)

        def settle(eng):
            eng.sem_inc(s_settled[eng.engine.name], 1)

        def tiles_of(array, k):
            return array[:, k * TPG:(k + 1) * TPG] if isinstance(k, int) else array[:, bass.ds(k * TPG, TPG)]

        def tile_at(array, k, i):
            t = k * TPG + i
            return array[:, bass.ds(t, 1)] if not isinstance(t, int) else array[:, t:t + 1]

        class Steps:

            def __init__(self, eng, s, turn, each):
                self.eng, self.s, self.turn, self.each, self.n = eng, s, turn, each, 0

            def did(self, ins):
                ins.then_inc(self.s, 1)
                self.n += 1

            def wait(self):
                self.eng.wait_ge(self.s, self.turn * self.each + self.n)

            def end(self):
                assert self.n == self.each, (self.n, self.each)

        def turns(eng, body):
            body(0)
            body(1)
            with eng.Fori(2, G - 1) as k:
                body(k)
            for k in range(G - 1, G + 2):
                body(k)

        def has(k, back):
            return not isinstance(k, int) or 0 <= k - back < G

        named = [0]

        def int_registers(eng, table, at, n, high):
            named[0] += 1
            regs = [eng.alloc_register(f"{table.name}_{named[0]}_{i}") for i in range(n)]
            eng.reg_load(regs, table[0:1, bass.ds(at, n)] if not isinstance(at, int) else table[0:1, at:at + n])
            out = [nc.s_assert_within(eng.snap(r), 0, high, skip_runtime_bounds_check_because="made from counts")
                   for r in regs]
            return out, regs

        def free_registers(eng, regs):
            for r in regs:
                eng.free_register(r)

        GATE_STEPS, SLOT_STEPS = 5, 2

        def bin_wait(eng, k):
            if not isinstance(k, int) or k > 2:
                eng.wait_ge(s_bin, 16 * K * TPG * (k - 2))

        block = ctx.enter_context(nc.Block())

        @block.sync
        def _(sp):
            x_v = x.rearrange("g (i p) d -> g p i d", p=P)
            adj_v = adj.rearrange("g (i p) j -> g p i j", p=P)
            sp.dma_start(x_sb[:, 0:TPG, :], x_v[0]).then_inc(s_x, 16)
            sp.dma_start(adj_sb[:, :, :], adj_v[0]).then_inc(s_adj, 16)
            sp.wait_ge(s_x, 16)
            sp.dma_start(x_sb[:, TPG:2 * TPG, :], x_v[1]).then_inc(s_x, 16)

            def load_adj(g):
                sp.wait_ge(s_mask, g)
                src = adj_v[g] if isinstance(g, int) else adj_v[bass.ds(g, 1)].rearrange("a p i j -> p (a i) j")
                sp.dma_start(adj_sb[:, :, :], src).then_inc(s_adj, 16)

            with sp.Fori(1, G - 1) as g:
                load_adj(g)
                sp.wait_ge(s_x, 16 * g + 16)
                sp.dma_start(x_sb[:, bass.ds((g + 1) * TPG, TPG), :],
                             x_v[bass.ds(g + 1, 1)].rearrange("a p i d -> p (a i) d")).then_inc(s_x, 16)
            load_adj(G - 1)
            sp.wait_ge(s_const, 1)
            sp.dma_start(bins[PAD_ROW:PAD_ROW + P, :], pad_rows[:, :]).then_inc(s_padrow, 16)
            sp.wait_ge(s_padrow, 16)
            sp.wait_ge(s_tab, 1)
            for e0 in range(0, E, 8):
                at, regs = int_registers(sp, base_i, e0, 8, PAD_ROW)
                for e in range(8):
                    sp.dma_start(bins[bass.ds(at[e], P), :], pad_rows[:, :]).then_inc(s_pad, 16)
                free_registers(sp, regs)
            sp.wait_ge(s_pad, 16 * E)
            sp.wait_ge(s_tab_done, 1)
            sp.wait_ge(s_bin, 16 * K * TILES)

            def loads(k):
                at, regs = int_registers(sp, first_row_i, k * TU, TU, PAD_ROW)
                for u in range(TU):
                    t = k * TU + u
                    wait_for(sp, s_tx, t - TU + 1)
                    wait_for(sp, s_y, t - TU + 1)
                    sp.dma_start(xg[:, u, :], bins[bass.ds(at[u], P), :]).then_inc(s_xg[u], 16)
                free_registers(sp, regs)

            loads(0)
            with sp.Fori(1, TURNS) as k:
                loads(k)
            for u in range(TU):
                sp.wait_ge(s_sc[u], 16 * TURNS)
            res_v = results.rearrange("(g i p k) d -> g p i (k d)", g=G, p=P, k=K)
            out_v = out.rearrange("g (i p) d -> g p i d", p=P)

            def load_results(h, b):
                g = h * 2 + b
                wait_for(sp, s_fn, g - 1)
                src = res_v[g] if isinstance(g, int) else res_v[bass.ds(g, 1)].rearrange("a p i d -> p (a i) d")
                sp.dma_start(yy[:, b, :, :], src).then_inc(s_yy[b], 16)

            def store(h, b):
                g = h * 2 + b
                wait_for(sp, s_fo, g + 1)
                dst = out_v[g] if isinstance(g, int) else out_v[bass.ds(g, 1)].rearrange("a p i d -> p (a i) d")
                sp.dma_start(dst, outn[:, b, :, :]).then_inc(s_out[b], 16)

            load_results(0, 0)
            load_results(0, 1)
            with sp.Fori(1, G // 2) as h:
                for b in range(2):
                    load_results(h, b)
                    store(h - 1, b)
            for b in range(2):
                store(G // 2 - 1, b)
            for b in range(2):
                sp.wait_ge(s_out[b], 16 * (G // 2))

        @block.gpsimd
        def _(pool):
            nc.gpsimd.memset(ident[:, :], 0.0)
            nc.gpsimd.memset(before_bf[:, :], 1.0)
            nc.gpsimd.memset(ones_bf[:, :], 1.0)
            nc.gpsimd.memset(half[:, :], -0.5)
            nc.gpsimd.memset(pad_rows[:, :], 0.0).then_inc(s_early, 1)
            pool.wait_ge(s_early, 1)
            nc.gpsimd.memset(pad_rows[:, D:D + 1], FAR)
            nc.gpsimd.affine_select(ident[:, :], ident[:, :], [[-1, P]], ALU.not_equal, 1.0, base=0,
                                    channel_multiplier=1)
            nc.gpsimd.affine_select(before_bf[:, :], before_bf[:, :], [[1, P]], ALU.is_gt, 0.0, base=0,
                                    channel_multiplier=-1).then_inc(s_early, 1)
            pool.wait_ge(s_early, 2)
            nc.gpsimd.tensor_copy(ident_bf[:, :], ident[:, :])
            nc.gpsimd.iota(expert_no[:, :], [[1, E]], base=0, channel_multiplier=0,
                           allow_small_or_imprecise_dtypes=True)
            nc.gpsimd.iota(bin_start[:, :], [[BIN, E]], base=0, channel_multiplier=0,
                           allow_small_or_imprecise_dtypes=True)
            nc.gpsimd.iota(base[:, :], [[BIN, E]], base=0, channel_multiplier=0,
                           allow_small_or_imprecise_dtypes=True)
            nc.gpsimd.iota(tile_no[:, :], [[1, XT]], base=0, channel_multiplier=0,
                           allow_small_or_imprecise_dtypes=True)
            nc.gpsimd.iota(token2[:, :], [[K * P, TILES]], base=0, channel_multiplier=K,
                           allow_small_or_imprecise_dtypes=True).then_inc(s_const, 1)

            def rstds(k):
                if has(k, -1):
                    pool.wait_ge(s_mv1, k + 2)
                if has(k, 1):
                    pool.wait_ge(s_mv2, k)
                settle(pool)
                nc.gpsimd.tensor_scalar(var_eps[:, :], mv[:, :, 1:2].rearrange("p a b -> p (a b)"), EPS, None,
                                        ALU.add).then_inc(s_pow, 1)
                pool.wait_ge(s_pow, k + 2)
                nc.gpsimd.tensor_tensor(rstd[:, :], var_eps[:, :], half[:, :], ALU.pow).then_inc(s_rs, 1)

            def scatter_rows(g):
                pool.wait_ge(s_slot, g + 1)
                pool.wait_ge(s_row_out, g + 1)
                settle(pool)
                for i in range(TPG):
                    for j in range(K):
                        nc.gpsimd.indirect_dma_start(bins, bass.IndirectOffsetOnAxis(ap=slots[:, i, j:j + 1], axis=0),
                                                     row_out[:, i, :], None).then_inc(s_bin, 16)

            def body(k):
                if has(k, -1) or has(k, 1):
                    rstds(k)
                if has(k, 2):
                    scatter_rows(k - 2)

            rstds(-1)
            turns(pool, body)

            def scatter_results(k):
                for u in range(TU):
                    pool.wait_ge(s_y, k * TU + u + 1)
                    settle(pool)
                    nc.gpsimd.indirect_dma_start(results, bass.IndirectOffsetOnAxis(ap=dest[:, u:u + 1], axis=0),
                                                 y[:, u, :], None, bounds_check=TOK * K - 1,
                                                 oob_is_err=False).then_inc(s_sc[u], 16)
            with pool.Fori(0, TURNS) as k:
                scatter_results(k)

            def final_rstd(g):
                pool.wait_ge(s_fmv, g + 1)
                settle(pool)
                nc.gpsimd.tensor_scalar(var_eps[:, 0:TPG], mv[:, 0:TPG, 1:2].rearrange("p a b -> p (a b)"), EPS, None,
                                        ALU.add).then_inc(s_pow, 1)
                pool.wait_ge(s_pow, g + G + 3)
                nc.gpsimd.tensor_tensor(rstd[:, 0:TPG], var_eps[:, 0:TPG], half[:, 0:TPG], ALU.pow).then_inc(s_frs, 1)
            with pool.Fori(0, G) as g:
                final_rstd(g)

        @block.scalar
        def _(act):
            def bcast(v, n):
                return v.rearrange("(a n) -> a n", a=1).to_broadcast((P, n))
            for dst, src in ((W_sb[:, :], W), (a12_sb[:, :], a_12), (a1_sb[:, :], a_1), (a2_sb[:, :], a_2),
                             (W21[:, 0:D], W_2), (W21[:, D:2 * D], W_1), (gate_sb[:, :], gate_w),
                             (b1_rows[:, :], b1.rearrange("e (c p) -> (e c) p", p=P)),
                             (gate_bias[:, :], bcast(gate_b, E))):
                act.dma_start(dst, src).then_inc(s_gnn_w, 16)
            act.dma_start(w1_sb[:, :].rearrange("p (e f) -> p e f", e=E), w1.rearrange("e p f -> p e f")).then_inc(s_late, 16)
            act.dma_start(w2_sb[:, :].rearrange("p (a d) -> p a d", d=D),
                          w2.rearrange("e (c p) d -> p (e c) d", p=P)).then_inc(s_late, 16)
            act.dma_start(b2_all[:, :], bcast(b2.rearrange("e d -> (e d)"), E * D)).then_inc(s_late, 16)
            act.dma_start(gamma_all[:, :], bcast(gamma, D)).then_inc(s_late, 16)
            act.dma_start(beta_all[:, :], bcast(beta, D)).then_inc(s_late, 16)
            act.preload_act_table(ACT.Exp)

            def pt_copy(k, i):
                n = (k - 1) * TPG + i
                act.wait_ge(s_pt, n + 1)
                wait_for(act, s_pv, n - 1)
                nc.scalar.copy(probT[:, 0, :], bank[2][:, :]).then_inc(s_pta, 1)

            def relu(k, i):
                act.wait_ge(s_s, k * TPG + i + 1)
                if i == 0:
                    act.wait_ge(s_ay, k + 1)
                nc.scalar.activation(relu4[:, i % 2, :], bank[i % 2][:, :], ACT.Relu, bias=tile_at(ay4, k, i),
                                     scale=4.0).then_inc(s_relu, 1)

            def exps(k, i):
                act.wait_ge(s_em, k * TPG + i + 1)
                nc.scalar.activation(prob[:, i, :], prob[:, i, :], ACT.Exp, bias=row_min[:, i:i + 1], scale=-1.0,
                                     accum_out=tile_at(row_sum, k, i)).then_inc(s_exp, 1)

            def body(k):
                if has(k, 0):
                    act.wait_ge(s_ft, k + 1)
                    wait_for(act, s_hv, 2 * k)
                    nc.scalar.copy(featT[:, :], bank[4][:, :]).then_inc(s_ft_sb, 1)
                    act.wait_ge(s_qt, k + 1)
                    wait_for(act, s_s, k * TPG)
                    nc.scalar.activation(qT[:, :], bank[5][:, :], ACT.Identity, bias=u1[:, :]).then_inc(s_qt_sb, 1)
                if has(k, 1):
                    pt_copy(k, 0)
                if has(k, 0):
                    relu(k, 0)
                    relu(k, 1)
                    exps(k, 0)
                if has(k, 1):
                    pt_copy(k, 2)
                if has(k, 0):
                    exps(k, 1)
                    relu(k, 2)
                    relu(k, 3)
                    exps(k, 2)
                if has(k, 2):
                    act.wait_ge(s_member, k - 1)
                    bin_wait(act, k)
                    nc.scalar.copy(row_out[:, :, :], row[:, :, :]).then_inc(s_row_out, 1)
                    nc.scalar.copy(tiles_of(xn_all, k - 2), row[:, :, 0:D]).then_inc(s_row_kept, 1)
                if has(k, 0):
                    exps(k, 3)
                    for pair in range(2):
                        act.wait_ge(s_hv, 2 * k + pair + 1)
                        if pair == 0:
                            wait_for(act, s_z, k)
                        nc.scalar.copy(vh[:, 2 * pair:2 * pair + 2, :].rearrange("p a b -> p (a b)"),
                                       bank[4 + pair][:, :]).then_inc(s_hv_sb, 1)
                if has(k, 1):
                    act.wait_ge(s_zneg, k)
                    nc.scalar.activation(zneg[:, :, :], zneg[:, :, :], ACT.Exp).then_inc(s_e, 1)
            act.wait_ge(s_wt_sb, 4)
            turns(act, body)

            act.wait_ge(s_gate, G * GATE_STEPS)
            nc.scalar.activation(wexp[:, :], gap[:, :], ACT.Exp).then_inc(s_gap, 1)

            def x_copy(t, u):
                act.wait_ge(s_tx, t + 1)
                wait_for(act, s_mm1, t - 1)
                nc.scalar.copy(xgT[:, u % 2, :], bank[u % 2][:, 0:P]).then_inc(s_xgt, 1)

            def ffn(k, last=False):
                for u in range(TU):
                    t = k * TU + u
                    act.wait_ge(s_mm1, t + 1)
                    wait_for(act, s_ht, t - 1)
                    nc.scalar.copy(hid[:, u % 2, :], bank[2 + u % 2][:, 0:F]).then_inc(s_h, 1)
                    if not (last and u + 2 >= TU):
                        x_copy(t + 2, u)
            x_copy(0, 0)
            x_copy(1, 1)
            ffn(0)
            with act.Fori(1, TURNS - 1) as k:
                ffn(k)
            ffn(TURNS - 1, last=True)

        @block.tensor
        def _(pe):
            mm = nc.tensor.matmul
            pe.wait_ge(s_const, 1)
            pe.wait_ge(s_gnn_w, 16 * 9)
            nc.tensor.transpose(bank[0][:, 0:P], W_sb[:, :], ident[:, :])
            nc.tensor.transpose(bank[0][:, P:2 * P], a12_sb[:, :], ident[:, :])
            nc.tensor.transpose(bank[0][:, 2 * P:2 * P + E * FC], b1_rows[:, :], ident[0:E * FC, 0:E * FC]).then_inc(s_wt, 1)
            pe.wait_ge(s_wt_sb, 3)
            mm(bank[1][:, 0:D], a12T[:, :], WT[:, :], start=True, stop=True)
            mm(bank[1][:, D:D + 1], WT[:, :], a1_sb[:, :], start=True, stop=True)
            mm(bank[1][:, D + 1:D + 2], WT[:, :], a2_sb[:, :], start=True, stop=True).then_inc(s_wt, 1)
            pe.wait_ge(s_wt_sb, 6)
            mm(bank[2][:, 0:D], WT[:, :], C_sb[:, :], start=True, stop=True).then_inc(s_wt, 1)
            pe.wait_ge(s_wt_sb, 7)

            def prob_transposes(k, i):
                n = (k - 1) * TPG + i
                pe.wait_ge(s_exp, n + 1)
                wait_for(pe, s_ptd if i % 2 else s_pta, (k - 1) * 2 + i // 2)
                for c in range(TPG):
                    last = nc.tensor.transpose(bank[2 + i % 2][:, c * P:(c + 1) * P], prob[:, i, c * P:(c + 1) * P],
                                               ident[:, :])
                last.then_inc(s_pt, 1)

            def scores(k, i):
                if i == 0:
                    pe.wait_ge(s_mask, k + 1)
                    pe.wait_ge(s_qt_sb, k + 1)
                wait_for(pe, s_em, k * TPG + i - 1)
                mm(bank[i % 2][:, :], ident_bf[:, :], no_edge[:, i, :], start=True, stop=False)
                mm(bank[i % 2][:, :], qT[:, i * P:(i + 1) * P], featT[:, :], start=False, stop=True).then_inc(s_s, 1)

            def values(k, i):
                if i == 0:
                    wait_for(pe, s_z, k - 1)
                    pe.wait_ge(s_hv_sb, 2 * k)
                pe.wait_ge(s_ptd if i % 2 else s_pta, (k - 1) * 2 + i // 2 + 1)
                for c in range(TPG):
                    last = mm(bank[6][:, i * P:(i + 1) * P], probT[:, i % 2, c * P:(c + 1) * P], vh[:, c, 0:D],
                              start=(c == 0), stop=(c == TPG - 1))
                last.then_inc(s_pv, 1)

            def body(k):
                if has(k, 0):
                    pe.wait_ge(s_feat, k + 1)
                    wait_for(pe, s_hv_sb, 2 * k - 1)
                    for i in range(TPG):
                        last = nc.tensor.transpose(bank[4][:, i * P:(i + 1) * P], feat[:, i, :], ident[:, :])
                    last.then_inc(s_ft, 1)
                if has(k, 2):
                    pe.wait_ge(s_x2n, k - 1)
                    pe.wait_ge(s_ay, min(k, G) if isinstance(k, int) else k)
                    wait_for(pe, s_slot, k - 2)
                    for i in range(TPG):
                        last = nc.tensor.transpose(bank[7][:, i * P:(i + 1) * P], row[:, i, 0:D], ident[:, :])
                    last.then_inc(s_x2t, 1)
                if has(k, 0):
                    pe.wait_ge(s_ft_sb, k + 1)
                    wait_for(pe, s_hv_sb, 2 * k)
                    mm(bank[5][:, :], M_sb[:, :], featT[:, :], start=True, stop=True).then_inc(s_qt, 1)
                if has(k, 0) or has(k, 2):
                    if has(k, 2):
                        pe.wait_ge(s_x2t_sb, k - 1)
                    else:
                        wait_for(pe, s_ay, k)
                    if has(k, 0):
                        for i in range(TPG):
                            last = mm(bank[7][:, i:i + 1], featT[:, i * P:(i + 1) * P], u2[:, :], start=True, stop=True)
                    if has(k, 2):
                        for i in range(TPG):
                            last = mm(bank[7][:, E * (i + 1):E * (i + 2)], x2T[:, i * P:(i + 1) * P], gate_sb[:, :],
                                      start=True, stop=True)
                    last.then_inc(s_small, 1)
                for i in range(TPG):
                    if has(k, 1):
                        prob_transposes(k, i)
                    if has(k, 0):
                        scores(k, i)
                    if has(k, 1):
                        values(k, i)
                    if i == 1 and has(k, 2):
                        pe.wait_ge(s_member, k - 1)
                        for a in range(TPG + 1):
                            o = bank[7][:, E * a:E * (a + 1)]
                            for c in range(a):
                                last = mm(o, ones_bf[:, :], member[:, c, :], start=(c == 0), stop=(a == TPG and c == a - 1))
                            if a < TPG:
                                last = mm(o, before_bf[:, :], member[:, a, :], start=(a == 0), stop=True)
                        last.then_inc(s_rank, 1)
                if has(k, 0):
                    for i in range(TPG):
                        last = mm(bank[4 + i // 2][:, (i % 2) * 2 * D:(i % 2 + 1) * 2 * D], featT[:, i * P:(i + 1) * P],
                                  W21[:, :], start=True, stop=True)
                        if i % 2:
                            last.then_inc(s_hv, 1)
            turns(pe, body)

            pe.wait_ge(s_late, 16 * 5)
            pe.wait_ge(s_tab_done, 1)

            def x_transpose(t, k, u):
                pe.wait_ge(s_xg[u], 16 * (k + 1))
                nc.tensor.transpose(bank[u % 2][:, 0:P], xg[:, u, 0:D], ident[:, :]).then_inc(s_tx, 1)

            def ffn(k, first=False, last=False):
                no, regs = int_registers(pe, expert_i, k * TU, TU + 1, E - 1)
                for u in range(TU):
                    t = k * TU + u
                    pe.wait_ge(s_xgt, t + 1)
                    wait_for(pe, s_h, t - 1)
                    mm(bank[2 + u % 2][:, 0:F], xgT[:, u % 2, :], w1_sb[:, bass.ds(no[u + 1] * F, F)], start=True,
                       stop=True).then_inc(s_mm1, 1)
                    if not (first and u == 0):
                        second(t - 1, (u + 1) % 2, no[u])
                    if not (last and u + 2 >= TU):
                        v = (u + 2) % TU
                        if u + 2 < TU:
                            x_transpose(t + 2, k, v)
                        else:
                            x_transpose(t + 2, k + 1, v)
                    pe.wait_ge(s_h, t + 1)
                    wait_for(pe, s_hr, t - 1)
                    for c in range(FC):
                        tr = nc.tensor.transpose(bank[4 + u % 2][:, c * P:(c + 1) * P], hid[:, u % 2, c * P:(c + 1) * P],
                                                 ident[:, :])
                    tr.then_inc(s_ht, 1)
                if last:
                    second(TURNS * TU - 1, (TU - 1) % 2, no[TU])
                free_registers(pe, regs)

            def second(t, b, e):
                pe.wait_ge(s_hr, t + 1)
                wait_for(pe, s_y, t - 1)
                for c in range(FC):
                    m2 = mm(bank[6 + b][:, 0:D], hidT[:, b, c * P:(c + 1) * P], w2_sb[:, bass.ds((e * FC + c) * D, D)],
                            start=(c == 0), stop=(c == FC - 1))
                m2.then_inc(s_mm2, 1)

            x_transpose(0, 0, 0)
            x_transpose(1, 0, 1)
            ffn(0, first=True)
            with pe.Fori(1, TURNS - 1) as k:
                ffn(k)
            ffn(TURNS - 1, last=True)

        @block.vector
        def _(dve):
            V = nc.vector
            setup = Steps(dve, s_wt_sb, 0, 7)
            dve.wait_ge(s_wt, 1)
            setup.did(V.tensor_copy(WT[:, :], bank[0][:, 0:P]))
            setup.did(V.tensor_copy(a12T[:, :], bank[0][:, P:2 * P]))
            setup.did(V.tensor_copy(b1_cols[:, :], bank[0][:, 2 * P:2 * P + E * FC]))
            dve.wait_ge(s_wt, 2)
            setup.did(V.tensor_copy(u1[:, :], bank[1][:, D:D + 1]))
            setup.did(V.tensor_copy(u2[:, :], bank[1][:, D + 1:D + 2]))
            setup.did(V.tensor_copy(C_sb[:, :], bank[1][:, 0:D]))
            dve.wait_ge(s_wt, 3)
            setup.did(V.tensor_copy(M_sb[:, :], bank[2][:, 0:D]))

            def xt(k, i):
                t = k * TPG + i
                return x_sb[:, t, :] if isinstance(t, int) else x_sb[:, bass.ds(t, 1), :].rearrange("p a d -> p (a d)")

            def xg_of(k):
                return x_sb[:, k * TPG:(k + 1) * TPG, :] if isinstance(k, int) else x_sb[:, bass.ds(k * TPG, TPG), :]

            def mask(k):
                dve.wait_ge(s_adj, 16 * (k + 1))
                wait_for(dve, s_s, k * TPG)
                V.tensor_scalar(no_edge[:, :, :], adj_sb[:, :, :], 0.0, NEG_INF, ALU.is_le, ALU.mult).then_inc(s_mask, 1)

            def stats(k, o, s_stats, s_made):
                settle(dve)
                for i in range(TPG):
                    last = V.bn_stats(bn[:, o + i, :], xt(k, i))
                last.then_inc(s_stats, 1)
                dve.wait_ge(s_stats, k + 1)
                settle(dve)
                for i in range(TPG):
                    last = V.bn_aggr(mv[:, o + i, :], bn[:, o + i, :])
                last.then_inc(s_made, 1)

            V.memset(mv[:, :, :], 1.0).then_inc(s_bn, 1)
            dve.wait_ge(s_bn, 1)
            dve.wait_ge(s_x, 16)
            stats(0, 0, s_bn1, s_mv1)
            mask(0)
            dve.wait_ge(s_rs, 1)
            for i in range(TPG):
                ins = V.tensor_scalar(feat[:, i, :], xt(0, i), mv[:, i, 0:1], rstd[:, i:i + 1], ALU.subtract, ALU.mult)
            ins.then_inc(s_feat, 1)

            def body(k):
                if has(k, 2):
                    dve.wait_ge(s_x2t, k - 1)
                    V.tensor_copy(x2T[:, :], bank[7][:, :]).then_inc(s_x2t_sb, 1)
                if has(k, 0) or has(k, 2):
                    dve.wait_ge(s_small, k + 1)
                if has(k, 0):
                    V.tensor_scalar(tiles_of(ay4, k), bank[7][:, 0:TPG], 4.0, None, ALU.mult).then_inc(s_ay, 1)
                if has(k, 2):
                    gate(k - 2)
                for i in range(TPG):
                    if has(k, 0):
                        dve.wait_ge(s_relu, k * TPG + i + 1)
                        wait_for(dve, s_pt, (k - 1) * TPG + i + 1)
                        settle(dve)
                        V.tensor_tensor_reduce(prob[:, i, :], bank[i % 2][:, :], relu4[:, i % 2, :], -ALPHA, 3e38,
                                               ALU.add, ALU.min, row_min[:, i:i + 1]).then_inc(s_em, 1)
                    if has(k, 1) and i % 2 == 0:
                        n = (k - 1) * TPG + i + 1
                        dve.wait_ge(s_pt, n + 1)
                        wait_for(dve, s_pv, n - 1)
                        V.tensor_copy(probT[:, 1, :], bank[3][:, :]).then_inc(s_ptd, 1)
                    if has(k, 2) and i == 1:
                        slot(k - 2)
                if has(k, 1):
                    zs = Steps(dve, s_zs, k - 1, 3)
                    dve.wait_ge(s_exp, k * TPG)
                    zs.did(V.reciprocal(rinv[:, :], tiles_of(row_sum, k - 1)))
                    zs.wait()
                    dve.wait_ge(s_pv, k * TPG)
                    for i in range(TPG):
                        last = V.scalar_tensor_tensor(out=z[:, i, :], in0=bank[6][:, i * P:(i + 1) * P],
                                                      scalar=rinv[:, i:i + 1], in1=vh[:, i, D:2 * D], op0=ALU.mult,
                                                      op1=ALU.add)
                    last.then_inc(s_z, 1)
                    dve.wait_ge(s_z, k)
                    V.tensor_scalar(zneg[:, :, :], z[:, :, :], 0.0, None, ALU.min).then_inc(s_zneg, 1)
                    zs.did(V.scalar_tensor_tensor(out=z[:, :, :].rearrange("p a b -> p (a b)"),
                                                  in0=z[:, :, :].rearrange("p a b -> p (a b)"), scalar=0.0,
                                                  in1=xg_of(k - 1).rearrange("p a b -> p (a b)"), op0=ALU.max, op1=ALU.add))
                if has(k, -1):
                    mask(k + 1)
                if has(k, -1):
                    dve.wait_ge(s_x, 16 * (k + 2))
                    stats(k + 1, 0, s_bn1, s_mv1)
                if has(k, 1):
                    dve.wait_ge(s_e, k)
                    zs.wait()
                    zs.did(V.scalar_tensor_tensor(out=xg_of(k - 1), in0=zneg[:, :, :], scalar=-1.0, in1=z[:, :, :],
                                                  op0=ALU.add, op1=ALU.add))
                    zs.wait()
                    zs.end()
                    stats(k - 1, TPG, s_bn2, s_mv2)
                if has(k, -1) or has(k, 1):
                    dve.wait_ge(s_rs, k + 2)
                if has(k, -1):
                    dve.wait_ge(s_ft, k + 1)
                    for i in range(TPG):
                        last = V.tensor_scalar(feat[:, i, :], xt(k + 1, i), mv[:, i, 0:1], rstd[:, i:i + 1],
                                               ALU.subtract, ALU.mult)
                    last.then_inc(s_feat, 1)
                if has(k, 1):
                    wait_for(dve, s_row_out, k - 1)
                    wait_for(dve, s_row_kept, k - 1)
                    for i in range(TPG):
                        last = V.tensor_scalar(row[:, i, 0:D], xt(k - 1, i), mv[:, TPG + i, 0:1],
                                               rstd[:, TPG + i:TPG + i + 1], ALU.subtract, ALU.mult)
                    last.then_inc(s_x2n, 1)

            def gate(g):
                s = Steps(dve, s_gate, g, GATE_STEPS)
                s.did(V.tensor_tensor(logit[:, :, :], bank[7][:, E:E + TPG * E].rearrange("p (a e) -> p a e", a=TPG),
                                      gate_bias[:, :].rearrange("p (a e) -> p a e", a=1).to_broadcast((P, TPG, E)), ALU.add))
                s.wait()
                settle(dve)
                for i in range(TPG):
                    last = V.max(top[:, i, :], logit[:, i, :])
                s.did(last)
                s.wait()
                settle(dve)
                for i in range(TPG):
                    V.max_index(top_no[:, i, :], top[:, i, :], logit[:, i, :])
                s.did(V.tensor_tensor(tiles_of(gap, g), top[:, :, 1:2].rearrange("p a b -> p (a b)"),
                                      top[:, :, 0:1].rearrange("p a b -> p (a b)"), ALU.subtract))
                s.wait()
                s.did(V.tensor_copy(chosen[:, :, :], top_no[:, :, 0:K]))
                s.wait()
                V.tensor_copy(row[:, :, D:D + 1].rearrange("p a b -> p (a b)"), tiles_of(token2, g))
                V.tensor_copy(row[:, :, D + 1:D + 2], chosen[:, :, 0:1])
                s.did(V.tensor_tensor(onehot[:, :, :],
                                      expert_no[:, :].rearrange("p (a e) -> p a e", a=1).to_broadcast((P, TPG * K, E)),
                                      chosen[:, :, :].rearrange("p a b -> p (a b)").rearrange("p (a b) -> p a b", b=1).to_broadcast((P, TPG * K, E)),
                                      ALU.is_equal))
                s.wait()
                oh = onehot[:, :, :].rearrange("p (a k) e -> p a k e", k=K)
                V.tensor_tensor(member[:, :, :], oh[:, :, 0, :], oh[:, :, 1, :], ALU.add).then_inc(s_member, 1)
                s.end()

            def slot(g):
                s = Steps(dve, s_slots, g, SLOT_STEPS)
                dve.wait_ge(s_rank, g + 1)
                s.did(V.tensor_tensor(place[:, :, :], bank[7][:, 0:TPG * E].rearrange("p (a e) -> p a e", a=TPG),
                                      base[:, :].rearrange("p (a e) -> p a e", a=1).to_broadcast((P, TPG, E)), ALU.add))
                s.wait()
                for j in range(K):
                    V.tensor_tensor(picked[:, :, :].rearrange("p (a k) e -> p a k e", k=K)[:, :, j, :],
                                          onehot[:, :, :].rearrange("p (a k) e -> p a k e", k=K)[:, :, j, :],
                                          place[:, :, :], ALU.mult)
                s.did(V.tensor_tensor(base[:, :], base[:, :], bank[7][:, TPG * E:(TPG + 1) * E], ALU.add))
                s.wait()
                bin_wait(dve, g + 2)
                with nc.allow_low_precision(reason="summed in float32; row numbers are whole"):
                    V.tensor_reduce(slots[:, :, :].rearrange("p a k -> p (a k)"), picked[:, :, :], AX_X,
                                    ALU.add).then_inc(s_slot, 1)
                s.end()

            dve.wait_ge(s_const, 1)
            turns(dve, body)

            tb = Steps(dve, s_tab, 0, 999)
            dve.wait_ge(s_slots, G * SLOT_STEPS)
            tb.did(V.tensor_copy(base_i[:, :], base[:, :]))
            tb.did(V.tensor_tensor(cnt[:, :], base[:, :], bin_start[:, :], ALU.subtract))
            tb.wait()
            tb.did(V.tensor_scalar(cnt_i[:, :], cnt[:, :], float(P - 1), None, ALU.add))
            tb.did(V.memset(scan[0][:, :], 0.0))
            tb.did(V.memset(scan[1][:, :], 0.0))
            tb.wait()
            tb.did(V.tensor_scalar(ntile_i[:, :], cnt_i[:, :], 7, None, ALU.logical_shift_right))
            tb.wait()
            tb.did(V.tensor_copy(scan[0][:, PADC:], ntile_i[:, :]))
            for n, by in enumerate((1, 2, 4, 8)):
                tb.wait()
                a, b = scan[n % 2], scan[1 - n % 2]
                tb.did(V.tensor_tensor(b[:, PADC:], a[:, PADC:], a[:, PADC - by:PADC + E - by], ALU.add))
            tb.wait()
            ends = scan[0][:, PADC:].rearrange("p (a e) -> p a e", a=1).to_broadcast((P, XT, E))
            tb.did(V.tensor_tensor(passed[:, :, :], ends,
                                   tile_no[:, :].rearrange("p (a e) -> p a e", e=1).to_broadcast((P, XT, E)), ALU.is_le))
            tb.wait()
            tb.did(V.tensor_reduce(expert_of[:, :], passed[:, :, :], AX_X, ALU.add))
            tb.wait()
            tb.did(V.tensor_tensor(passed[:, :, :], passed[:, :, :], ends, ALU.mult))
            tb.wait()
            tb.did(V.tensor_reduce(start_of[:, :], passed[:, :, :], AX_X, ALU.max))
            tb.did(V.tensor_scalar(expert_w[:, :], expert_of[:, :], float(E - 1), None, ALU.min))
            tb.did(V.tensor_scalar(first_row[:, :], expert_of[:, :], float(BIN), None, ALU.mult))
            tb.did(V.memset(expert_i[:, 0:1], 0))
            tb.wait()
            tb.did(V.tensor_copy(expert_i[:, 1:], expert_w[:, :]))
            tb.did(V.tensor_tensor(start_of[:, :], tile_no[:, :], start_of[:, :], ALU.subtract))
            tb.wait()
            tb.did(V.scalar_tensor_tensor(out=first_row[:, :], in0=start_of[:, :], scalar=float(P), in1=first_row[:, :],
                                          op0=ALU.mult, op1=ALU.add))
            tb.wait()
            V.tensor_scalar(first_row_i[:, :], first_row[:, :], float(PAD_ROW), None, ALU.min).then_inc(s_tab_done, 1)

            dve.wait_ge(s_late, 16 * 5)
            dve.wait_ge(s_tab_done, 1)

            def out_of(t, u, e, tn):
                dve.wait_ge(s_mm2, t + 1)
                wait_for(dve, s_sc[u], 16 * tn)
                V.scalar_tensor_tensor(out=dest[:, u:u + 1], in0=xg[:, u, D + 1:D + 2],
                                       scalar=expert_of[:, t:t + 1] if isinstance(t, int) else expert_of[:, bass.ds(t, 1)],
                                       in1=xg[:, u, D:D + 1], op0=ALU.not_equal, op1=ALU.add)
                V.tensor_tensor(y[:, u, :], bank[6 + u % 2][:, 0:D], b2_all[:, bass.ds(e * D, D)], ALU.add).then_inc(s_y, 1)

            def ffn(k, first=False, last=False):
                no, regs = int_registers(dve, expert_i, k * TU, TU + 1, E - 1)
                for u in range(TU):
                    t = k * TU + u
                    dve.wait_ge(s_ht, t + 1)
                    wait_for(dve, s_mm2, t - 1)
                    for c in range(FC):
                        r = V.tensor_scalar(hidT[:, u % 2, c * P:(c + 1) * P], bank[4 + u % 2][:, c * P:(c + 1) * P],
                                            b1_cols[:, bass.ds(no[u + 1] * FC + c, 1)], 0.0, ALU.add, ALU.max)
                    r.then_inc(s_hr, 1)
                    if u:
                        out_of(t - 1, u - 1, no[u], k)
                    elif not first:
                        out_of(t - 1, TU - 1, no[0], k - 1)
                if last:
                    out_of(TURNS * TU - 1, TU - 1, no[TU], TURNS - 1)
                free_registers(dve, regs)
            ffn(0, first=True)
            ffn(1)
            with dve.Fori(2, TURNS - 1) as k:
                ffn(k)
            ffn(TURNS - 1, last=True)

            dve.wait_ge(s_gap, 1)
            V.tensor_scalar(wsum[:, :], wexp[:, :], 1.0, None, ALU.add).then_inc(s_w, 1)
            dve.wait_ge(s_w, 1)
            V.reciprocal(wt[:, 0, :], wsum[:, :]).then_inc(s_w, 1)
            dve.wait_ge(s_w, 2)
            V.tensor_tensor(wt[:, 1, :], wexp[:, :], wt[:, 0, :], ALU.mult).then_inc(s_w, 1)
            dve.wait_ge(s_w, 3)

            def final(h, b):
                g = 2 * h + b
                s = Steps(dve, s_fin, g, 4 * TPG + 2)
                dve.wait_ge(s_yy[b], 16 * (h + 1))
                for j in range(K):
                    if j:
                        s.wait()
                    for i in range(TPG):
                        t = g * TPG + i
                        wc = wt[:, j, t:t + 1] if isinstance(t, int) else wt[:, j, bass.ds(t, 1)]
                        prev = acc[:, i, :] if j else (xn_all[:, t, :] if isinstance(t, int) else xn_all[:, bass.ds(t, 1), :].rearrange("p a d -> p (a d)"))
                        ins = V.scalar_tensor_tensor(out=acc[:, i, :], in0=yy[:, b, i, j * D:(j + 1) * D], scalar=wc,
                                                     in1=prev, op0=ALU.mult, op1=ALU.add)
                        if j == K - 1 and i == TPG - 1:
                            ins.then_inc(s_fn, 1)
                        elif j == 0:
                            s.did(ins)
                dve.wait_ge(s_fn, g + 1)
                settle(dve)
                for i in range(TPG):
                    s.did(V.bn_stats(bn[:, i, :], acc[:, i, :]))
                s.wait()
                settle(dve)
                for i in range(TPG):
                    s.did(V.bn_aggr(mv[:, i, :], bn[:, i, :]))
                s.wait()
                V.memset(bn[:, 0, 0:1], 0.0).then_inc(s_fmv, 1)
                dve.wait_ge(s_frs, g + 1)
                for i in range(TPG):
                    s.did(V.tensor_scalar(acc[:, i, :], acc[:, i, :], mv[:, i, 0:1], rstd[:, i:i + 1], ALU.subtract, ALU.mult))
                s.wait()
                wait_for(dve, s_out[b], 16 * h)
                s.did(V.tensor_tensor(outn[:, b, :, :], acc[:, :, :],
                                      gamma_all[:, :].rearrange("p (a d) -> p a d", a=1).to_broadcast((P, TPG, D)), ALU.mult))
                s.wait()
                s.did(V.tensor_tensor(outn[:, b, :, :], outn[:, b, :, :],
                                      beta_all[:, :].rearrange("p (a d) -> p a d", a=1).to_broadcast((P, TPG, D)), ALU.add))
                s.wait()
                V.tensor_tensor(outn[:, b, :, :], outn[:, b, :, :], xg_of(g), ALU.add).then_inc(s_fo, 1)
                s.end()
            for b in range(2):
                final(0, b)
            with dve.Fori(1, G // 2) as h:
                for b in range(2):
                    final(h, b)


_INS = ["x", "adj", "L0_gnn_W", "L0_gnn_a_1", "L0_gnn_a_2", "L0_gnn_a_12", "L0_gnn_W_1", "L0_gnn_W_2", "L0_ffn_gate_w",
        "L0_ffn_gate_b", "L0_ffn_w1", "L0_ffn_b1", "L0_ffn_w2", "L0_ffn_b2", "L0_ffn_gamma", "L0_ffn_beta"]


def kernel(**inputs):
    import numpy as _np
    import concourse.bacc as _bacc
    from concourse import mybir as _mybir
    from concourse.bass_utils import run_bass_kernel_spmd as _run

    nc = _bacc.Bacc("TRN2", target_bir_lowering=False, num_devices=1)
    arrays, args = {}, []
    for name in _INS:
        a = _np.ascontiguousarray(inputs[name])
        arrays[f"in_{name}_dram"] = a
        args.append(nc.dram_tensor(f"in_{name}_dram", a.shape, _mybir.dt.from_np(a.dtype), kind="ExternalInput").ap())
    out = nc.dram_tensor("out_0_dram", arrays["in_x_dram"].shape, _mybir.dt.float32, kind="ExternalOutput").ap()
    graph_attention_and_routed_experts(nc, *args, out)
    r = _run(nc, [arrays], core_ids=[0])
    return r.results[0]["out_0_dram"]
```

```python
from contextlib import ExitStack

import concourse.bass as bass
from concourse import mybir

F32 = mybir.dt.float32
BF16 = mybir.dt.bfloat16
I32 = mybir.dt.int32
U32 = mybir.dt.uint32
ALU = mybir.AluOpType
ACT = mybir.ActivationFunctionType
AX_X = mybir.AxisListType.X

P = 128
ALPHA = 0.2
NEG_INF = -9e15
EPS = 1e-5
FAR = float(1 << 20)


def graph_attention_and_routed_experts(nc, x, adj, W, a_1, a_2, a_12, W_1, W_2, gate_w, gate_b, w1, b1, w2, b2,
                                       gamma, beta, out):
    G, N, D = x.shape
    TPG = N // P
    TILES = G * TPG
    TOK = G * N
    E, _, F = w1.shape
    FC = F // P
    K = 2
    assert D == P and N == 512 and FC == 2 and E == 16

    META = 2
    ROW = D + META
    BIN = TOK + P
    PAD_ROW = E * BIN
    TU = 8
    XT = TOK * K // P + E
    assert XT % TU == 0
    TURNS = XT // TU
    BEFORE = 2

    bins = nc.dram_tensor("expert_bins", (PAD_ROW + P, ROW), F32, kind="Internal").ap()
    results = nc.dram_tensor("expert_results", (TOK * K, D), F32, kind="Internal").ap()

    with ExitStack() as ctx:
        def sb(name, shape, dt=F32):
            return ctx.enter_context(nc.sbuf_tensor(name, shape, dt))

        def sem(name):
            return ctx.enter_context(nc.semaphore(name))

        bank = [ctx.enter_context(nc.psum_tensor(f"bank{i}", [P, 512], F32)) for i in range(8)]

        ident = sb("ident", [P, P])
        ident_bf = sb("ident_bf", [P, P], BF16)
        ones_bf = sb("ones_bf", [P, P], BF16)
        before_bf = sb("before_bf", [P, P], BF16)
        expert_no = sb("expert_no", [P, E])
        bin_start = sb("bin_start", [P, E])
        tile_no = sb("tile_no", [P, XT])
        half = sb("half", [P, 2 * TPG])
        pad_rows = sb("pad_rows", [P, ROW])
        W_sb = sb("W_sb", [P, D])
        a12_sb = sb("a12_sb", [P, D])
        a1_sb = sb("a1_sb", [P, 1])
        a2_sb = sb("a2_sb", [P, 1])
        WT = sb("WT", [P, D])
        a12T = sb("a12T", [P, D])
        C_sb = sb("C_sb", [P, D])
        M_sb = sb("M_sb", [P, D])
        u1 = sb("u1", [P, 1])
        u2 = sb("u2", [P, 1])
        W21 = sb("W21", [P, 2 * D])
        gate_sb = sb("gate_sb", [P, E])
        gate_bias = sb("gate_bias", [P, E])
        w1_sb = sb("w1_sb", [P, E * F])
        w2_sb = sb("w2_sb", [P, E * FC * D])
        b1_rows = sb("b1_rows", [E * FC, P])
        b1_cols = sb("b1_cols", [P, E * FC])
        b2_all = sb("b2_all", [P, E * D])
        gamma_all = sb("gamma_all", [P, D])
        beta_all = sb("beta_all", [P, D])

        x_sb = sb("x_sb", [P, TILES, D])
        xn_all = sb("xn_all", [P, TILES, D])
        token2 = sb("token2", [P, TILES])
        ay4 = sb("ay4", [P, TILES])
        row_min = sb("row_min", [P, TPG])
        row_sum = sb("row_sum", [P, TILES])
        gap = sb("gap", [P, TILES])

        with ExitStack() as graph_only:
            adj_sb = graph_only.enter_context(nc.sbuf_tensor("adj_sb", [P, TPG, N], I32))
            no_edge = graph_only.enter_context(nc.sbuf_tensor("no_edge", [P, TPG, N], BF16))
            prob = graph_only.enter_context(nc.sbuf_tensor("prob", [P, TPG, N], F32))
        yy = sb("yy", [P, 2, TPG, K * D])
        acc = sb("acc", [P, 2, TPG, D])
        outn = sb("outn", [P, 2, TPG, D])
        fill = sb("fill", [P, 2 * N])
        feat = sb("feat", [P, TPG, D])
        featT = sb("featT", [P, N])
        qT = sb("qT", [P, N])
        vh = sb("vh", [P, TPG, 2 * D])
        relu4 = sb("relu4", [P, 2, N])
        probT = sb("probT", [P, 2, N])
        z = sb("z", [P, TPG, D])
        zneg = sb("zneg", [P, TPG, D])
        rinv = sb("rinv", [P, TPG])
        bn = sb("bn", [P, 2 * TPG, 6])
        mv = sb("mv", [P, 2 * TPG, 2])
        var_eps = sb("var_eps", [P, 2 * TPG])
        rstd = sb("rstd", [P, 2 * TPG])
        row = sb("row", [P, TPG, ROW])
        row_out = sb("row_out", [P, TPG, ROW])
        slots = sb("slots", [P, TPG, K], U32)
        x2T = sb("x2T", [P, N])
        logit = sb("logit", [P, TPG, E])
        top = sb("top", [P, TPG, 8])
        top_no = sb("top_no", [P, TPG, 8], U32)
        chosen = sb("chosen", [P, TPG, K])
        onehot = sb("onehot", [P, TPG * K, E])
        member = sb("member", [P, TPG, E], BF16)
        base = sb("base", [P, E])
        place = sb("place", [P, TPG, E])
        picked = sb("picked", [P, TPG * K, E])

        base_i = sb("base_i", [P, E], I32)
        cnt = sb("cnt", [P, E])
        cnt_i = sb("cnt_i", [P, E], I32)
        ntile_i = sb("ntile_i", [P, E], I32)
        PADC = 8
        scan = [sb(f"scan{i}", [P, PADC + E]) for i in range(2)]
        passed = sb("passed", [P, XT, E])
        expert_of = sb("expert_of", [P, XT])
        start_of = sb("start_of", [P, XT])
        first_row = sb("first_row", [P, XT])
        first_row_i = sb("first_row_i", [P, XT], I32)
        expert_w = sb("expert_w", [P, XT])
        expert_i = sb("expert_i", [P, BEFORE + XT + 1], I32)

        xg = sb("xg", [P, TU, ROW])
        xgT = sb("xgT", [P, 2, P])
        w1_cur = sb("w1_cur", [P, 4, F])
        hidT = sb("hidT", [P, 4, F])
        y = sb("y", [P, TU, D])
        dest = sb("dest", [P, TU], U32)

        wexp = sb("wexp", [P, TILES])
        wsum = sb("wsum", [P, TILES])
        wt = sb("wt", [P, K, TILES])

        s_early, s_gnn_w, s_late, s_const = sem("early_loaded"), sem("gnn_weights_loaded"), sem("late_loaded"), sem("constants_made")
        s_wt, s_wt_sb = sem("setup_matmul_done"), sem("setup_copied")
        s_x, s_adj = sem("x_loaded"), sem("adj_loaded")
        s_mask = sem("mask_made")
        s_bn, s_bn1, s_bn2 = sem("first_stats_made"), sem("feat_stats_made"), sem("row_stats_made")
        s_mv1, s_mv2 = sem("feat_variances_made"), sem("row_variances_made")
        s_rs1, s_rs2 = sem("feat_rstd_made"), sem("row_rstd_made")
        s_row_out, s_row_kept, s_slots = sem("row_out_copied"), sem("row_kept"), sem("slot_steps")
        s_pow = [sem("feat_rstd_step"), sem("row_rstd_step")]
        s_feat, s_x2n = sem("feat_made"), sem("rows_made")
        s_ft, s_ft_sb = sem("featT_done"), sem("featT_copied")
        s_qt, s_qt_sb = sem("qT_done"), sem("qT_copied")
        s_small, s_ay, s_logit = sem("ay_done"), sem("ay_copied"), sem("logits_done")
        s_hv, s_hv_sb = sem("vh_done"), sem("vh_copied")
        s_s, s_relu, s_em, s_exp = sem("scores_done"), sem("relu_made"), sem("masked_logits_made"), sem("prob_made")
        s_pt, s_pta, s_ptd = sem("probT_done"), sem("probT_even_copied"), sem("probT_odd_copied")
        s_pv, s_z, s_zneg, s_e = sem("pv_done"), sem("z_made"), sem("zneg_made"), sem("elu_exp_made")
        s_zs = sem("z_steps")
        s_x2t, s_x2t_sb = sem("x2T_done"), sem("x2T_copied")
        s_gate = sem("gate_steps")
        s_member, s_rank, s_slot = sem("member_made"), sem("rank_done"), sem("slots_made")
        s_bin = sem("rows_in_bins")
        s_tab, s_tab_done, s_pad = sem("table_steps"), sem("table_made"), sem("padding_written")
        s_padrow = sem("pad_tile_written")
        s_xg = [sem(f"tokens_loaded_{u}") for u in range(TU)]
        s_tx, s_xgt = sem("xgT_done"), sem("xgT_copied")
        s_wc, s_mm1, s_hr = sem("w1_copied"), sem("hidden_done"), sem("hidden_relu_made")
        s_mm2, s_y = sem("expert_out_done"), sem("expert_out_made")
        s_sc = [sem(f"results_scattered_{u}") for u in range(TU)]
        s_gap, s_w = sem("gate_exp_made"), sem("weight_steps")
        s_yy = [sem(f"results_loaded_{u}") for u in range(2)]
        s_fin, s_fmv, s_frs, s_fn, s_fo = sem("final_steps"), sem("final_var"), sem("final_rstd"), sem("final_scaled"), sem("final_made")
        s_out = [sem(f"out_stored_{u}") for u in range(2)]

        s_settled = {name: sem(f"waited_{name}") for name in ("Pool", "DVE")}

        def wait_for(eng, s, value):
            if not isinstance(value, int) or value > 0:
                eng.wait_ge(s, value)

        def settle(eng):
            eng.sem_inc(s_settled[eng.engine.name], 1)

        def tiles_of(array, k):
            return array[:, k * TPG:(k + 1) * TPG] if isinstance(k, int) else array[:, bass.ds(k * TPG, TPG)]

        def tile_at(array, k, i):
            t = k * TPG + i
            return array[:, bass.ds(t, 1)] if not isinstance(t, int) else array[:, t:t + 1]

        class Steps:

            def __init__(self, eng, s, turn, each):
                self.eng, self.s, self.turn, self.each, self.n = eng, s, turn, each, 0

            def did(self, ins):
                ins.then_inc(self.s, 1)
                self.n += 1

            def wait(self):
                self.eng.wait_ge(self.s, self.turn * self.each + self.n)

            def end(self):
                assert self.n == self.each, (self.n, self.each)

        def turns(eng, body):
            for k in range(3):
                body(k)
            with eng.Fori(3, G - 1) as k:
                body(k)
            for k in range(G - 1, G + 3):
                body(k)

        def has(k, back):
            return not isinstance(k, int) or 0 <= k - back < G

        named = [0]

        def int_registers(eng, table, at, n, high):
            named[0] += 1
            regs = [eng.alloc_register(f"{table.name}_{named[0]}_{i}") for i in range(n)]
            eng.reg_load(regs, table[0:1, bass.ds(at, n)] if not isinstance(at, int) else table[0:1, at:at + n])
            out = [nc.s_assert_within(eng.snap(r), 0, high, skip_runtime_bounds_check_because="made from counts")
                   for r in regs]
            return out, regs

        def free_registers(eng, regs):
            for r in regs:
                eng.free_register(r)

        GATE_STEPS, SLOT_STEPS = 5, 2

        def bin_wait(eng, g):
            if not isinstance(g, int) or g > 0:
                eng.wait_ge(s_bin, 16 * K * TPG * g)

        block = ctx.enter_context(nc.Block())

        @block.sync
        def _(sp):
            x_v = x.rearrange("g (i p) d -> g p i d", p=P)
            adj_v = adj.rearrange("g (i p) j -> g p i j", p=P)
            sp.dma_start(x_sb[:, 0:TPG, :], x_v[0]).then_inc(s_x, 16)
            sp.dma_start(adj_sb[:, :, :], adj_v[0]).then_inc(s_adj, 16)
            sp.wait_ge(s_x, 16)
            sp.dma_start(x_sb[:, TPG:2 * TPG, :], x_v[1]).then_inc(s_x, 16)

            def load_adj(g):
                sp.wait_ge(s_mask, g)
                src = adj_v[g] if isinstance(g, int) else adj_v[bass.ds(g, 1)].rearrange("a p i j -> p (a i) j")
                sp.dma_start(adj_sb[:, :, :], src).then_inc(s_adj, 16)

            with sp.Fori(1, G - 1) as g:
                load_adj(g)
                sp.wait_ge(s_x, 16 * g + 16)
                sp.dma_start(x_sb[:, bass.ds((g + 1) * TPG, TPG), :],
                             x_v[bass.ds(g + 1, 1)].rearrange("a p i d -> p (a i) d")).then_inc(s_x, 16)
            load_adj(G - 1)
            sp.wait_ge(s_const, 1)
            sp.dma_start(bins[PAD_ROW:PAD_ROW + P, :], pad_rows[:, :]).then_inc(s_padrow, 16)
            sp.wait_ge(s_padrow, 16)
            sp.wait_ge(s_tab, 1)
            for e0 in range(0, E, 8):
                at, regs = int_registers(sp, base_i, e0, 8, PAD_ROW)
                for e in range(8):
                    sp.dma_start(bins[bass.ds(at[e], P), :], pad_rows[:, :]).then_inc(s_pad, 16)
                free_registers(sp, regs)
            sp.wait_ge(s_pad, 16 * E)
            sp.wait_ge(s_tab_done, 1)
            sp.wait_ge(s_bin, 16 * K * TILES)

            def loads(k):
                at, regs = int_registers(sp, first_row_i, k * TU, TU, PAD_ROW)
                for u in range(TU):
                    t = k * TU + u
                    wait_for(sp, s_tx, t - TU + 1)
                    wait_for(sp, s_y, t - TU + 1)
                    sp.dma_start(xg[:, u, :], bins[bass.ds(at[u], P), :]).then_inc(s_xg[u], 16)
                free_registers(sp, regs)

            loads(0)
            with sp.Fori(1, TURNS) as k:
                loads(k)
            for u in range(TU):
                sp.wait_ge(s_sc[u], 16 * TURNS)
            res_v = results.rearrange("(g i p k) d -> g p i (k d)", g=G, p=P, k=K)
            out_v = out.rearrange("g (i p) d -> g p i d", p=P)

            def load_results(h, b):
                g = h * 2 + b
                wait_for(sp, s_fn, g - 1)
                src = res_v[g] if isinstance(g, int) else res_v[bass.ds(g, 1)].rearrange("a p i d -> p (a i) d")
                sp.dma_start(yy[:, b, :, :], src).then_inc(s_yy[b], 16)

            def store(h, b):
                g = h * 2 + b
                wait_for(sp, s_fo, g + 1)
                dst = out_v[g] if isinstance(g, int) else out_v[bass.ds(g, 1)].rearrange("a p i d -> p (a i) d")
                sp.dma_start(dst, outn[:, b, :, :]).then_inc(s_out[b], 16)

            load_results(0, 0)
            load_results(0, 1)
            with sp.Fori(1, G // 2) as h:
                for b in range(2):
                    load_results(h, b)
                    store(h - 1, b)
            for b in range(2):
                store(G // 2 - 1, b)
            for b in range(2):
                sp.wait_ge(s_out[b], 16 * (G // 2))

        @block.gpsimd
        def _(pool):
            nc.gpsimd.memset(ident[:, :], 0.0)
            nc.gpsimd.memset(before_bf[:, :], 1.0)
            nc.gpsimd.memset(ones_bf[:, :], 1.0)
            nc.gpsimd.memset(half[:, :], -0.5)
            nc.gpsimd.memset(pad_rows[:, :], 0.0).then_inc(s_early, 1)
            pool.wait_ge(s_early, 1)
            nc.gpsimd.memset(pad_rows[:, D:D + 1], FAR)
            nc.gpsimd.affine_select(ident[:, :], ident[:, :], [[-1, P]], ALU.not_equal, 1.0, base=0,
                                    channel_multiplier=1)
            nc.gpsimd.affine_select(before_bf[:, :], before_bf[:, :], [[1, P]], ALU.is_gt, 0.0, base=0,
                                    channel_multiplier=-1).then_inc(s_early, 1)
            pool.wait_ge(s_early, 2)
            nc.gpsimd.tensor_copy(ident_bf[:, :], ident[:, :])
            nc.gpsimd.iota(expert_no[:, :], [[1, E]], base=0, channel_multiplier=0,
                           allow_small_or_imprecise_dtypes=True)
            nc.gpsimd.iota(bin_start[:, :], [[BIN, E]], base=0, channel_multiplier=0,
                           allow_small_or_imprecise_dtypes=True)
            nc.gpsimd.iota(base[:, :], [[BIN, E]], base=0, channel_multiplier=0,
                           allow_small_or_imprecise_dtypes=True)
            nc.gpsimd.iota(tile_no[:, :], [[1, XT]], base=0, channel_multiplier=0,
                           allow_small_or_imprecise_dtypes=True)
            nc.gpsimd.iota(token2[:, :], [[K * P, TILES]], base=0, channel_multiplier=K,
                           allow_small_or_imprecise_dtypes=True).then_inc(s_const, 1)

            def rstds(o, n, made, done):
                pool.wait_ge(made, n)
                settle(pool)
                nc.gpsimd.tensor_scalar(var_eps[:, o:o + TPG], mv[:, o:o + TPG, 1:2].rearrange("p a b -> p (a b)"), EPS,
                                        None, ALU.add).then_inc(s_pow[o // TPG], 1)
                pool.wait_ge(s_pow[o // TPG], n)
                nc.gpsimd.tensor_tensor(rstd[:, o:o + TPG], var_eps[:, o:o + TPG], half[:, o:o + TPG],
                                        ALU.pow).then_inc(done, 1)

            def scatter_rows(g):
                pool.wait_ge(s_slot, g + 1)
                pool.wait_ge(s_row_out, g + 1)
                settle(pool)
                for i in range(TPG):
                    for j in range(K):
                        nc.gpsimd.indirect_dma_start(bins, bass.IndirectOffsetOnAxis(ap=slots[:, i, j:j + 1], axis=0),
                                                     row_out[:, i, :], None).then_inc(s_bin, 16)

            def body(k):
                if has(k, -1):
                    rstds(0, k + 2, s_mv1, s_rs1)
                if has(k, 3):
                    scatter_rows(k - 3)
                if has(k, 1):
                    rstds(TPG, k, s_mv2, s_rs2)

            rstds(0, 1, s_mv1, s_rs1)
            turns(pool, body)

            def scatter_results(k):
                for u in range(TU):
                    pool.wait_ge(s_y, k * TU + u + 1)
                    settle(pool)
                    nc.gpsimd.indirect_dma_start(results, bass.IndirectOffsetOnAxis(ap=dest[:, u:u + 1], axis=0),
                                                 y[:, u, :], None, bounds_check=TOK * K - 1,
                                                 oob_is_err=False).then_inc(s_sc[u], 16)
            with pool.Fori(0, TURNS) as k:
                scatter_results(k)

            def final_rstd(g):
                pool.wait_ge(s_fmv, g + 1)
                settle(pool)
                nc.gpsimd.tensor_scalar(var_eps[:, 0:TPG], mv[:, 0:TPG, 1:2].rearrange("p a b -> p (a b)"), EPS, None,
                                        ALU.add).then_inc(s_pow[0], 1)
                pool.wait_ge(s_pow[0], g + G + 1)
                nc.gpsimd.tensor_tensor(rstd[:, 0:TPG], var_eps[:, 0:TPG], half[:, 0:TPG], ALU.pow).then_inc(s_frs, 1)
            with pool.Fori(0, G) as g:
                final_rstd(g)

        @block.scalar
        def _(act):
            def bcast(v, n):
                return v.rearrange("(a n) -> a n", a=1).to_broadcast((P, n))
            for dst, src in ((W_sb[:, :], W), (a12_sb[:, :], a_12), (a1_sb[:, :], a_1), (a2_sb[:, :], a_2),
                             (W21[:, 0:D], W_2), (W21[:, D:2 * D], W_1), (gate_sb[:, :], gate_w),
                             (b1_rows[:, :], b1.rearrange("e (c p) -> (e c) p", p=P)),
                             (gate_bias[:, :], bcast(gate_b, E))):
                act.dma_start(dst, src).then_inc(s_gnn_w, 16)
            act.dma_start(w1_sb[:, :].rearrange("p (e f) -> p e f", e=E), w1.rearrange("e p f -> p e f")).then_inc(s_late, 16)
            act.dma_start(w2_sb[:, :].rearrange("p (a d) -> p a d", d=D),
                          w2.rearrange("e (c p) d -> p (e c) d", p=P)).then_inc(s_late, 16)
            act.dma_start(b2_all[:, :], bcast(b2.rearrange("e d -> (e d)"), E * D)).then_inc(s_late, 16)
            act.dma_start(gamma_all[:, :], bcast(gamma, D)).then_inc(s_late, 16)
            act.dma_start(beta_all[:, :], bcast(beta, D)).then_inc(s_late, 16)
            act.preload_act_table(ACT.Exp)

            def pt_copy(k, i):
                n = (k - 1) * TPG + i
                act.wait_ge(s_pt, n + 1)
                wait_for(act, s_pv, n - 1)
                nc.scalar.copy(probT[:, 0, :], bank[2][:, :]).then_inc(s_pta, 1)

            def relu(k, i):
                act.wait_ge(s_s, k * TPG + i + 1)
                if i == 0:
                    act.wait_ge(s_ay, k + 1)
                nc.scalar.activation(relu4[:, i % 2, :], bank[i % 2][:, :], ACT.Relu, bias=tile_at(ay4, k, i),
                                     scale=4.0).then_inc(s_relu, 1)

            def exps(k, i):
                act.wait_ge(s_em, k * TPG + i + 1)
                nc.scalar.activation(prob[:, i, :], prob[:, i, :], ACT.Exp, bias=row_min[:, i:i + 1], scale=-1.0,
                                     accum_out=tile_at(row_sum, k, i)).then_inc(s_exp, 1)

            def body(k):
                if has(k, 0):
                    act.wait_ge(s_ft, k + 1)
                    wait_for(act, s_hv, 2 * k)
                    nc.scalar.copy(featT[:, :], bank[4][:, :]).then_inc(s_ft_sb, 1)
                    act.wait_ge(s_qt, k + 1)
                    wait_for(act, s_s, k * TPG)
                    nc.scalar.activation(qT[:, :], bank[5][:, :], ACT.Identity, bias=u1[:, :]).then_inc(s_qt_sb, 1)
                if has(k, 1):
                    pt_copy(k, 0)
                if has(k, 0):
                    relu(k, 0)
                    relu(k, 1)
                    exps(k, 0)
                if has(k, 2):
                    act.wait_ge(s_x2t, k - 1)
                    nc.scalar.copy(x2T[:, :], bank[7][:, :]).then_inc(s_x2t_sb, 1)
                if has(k, 1):
                    pt_copy(k, 2)
                if has(k, 0):
                    exps(k, 1)
                    relu(k, 2)
                    relu(k, 3)
                    exps(k, 2)
                if has(k, 2):
                    act.wait_ge(s_member, k - 1)
                    bin_wait(act, k - 2)
                    nc.scalar.copy(row_out[:, :, :], row[:, :, :]).then_inc(s_row_out, 1)
                    nc.scalar.copy(tiles_of(xn_all, k - 2), row[:, :, 0:D]).then_inc(s_row_kept, 1)
                if has(k, 0):
                    exps(k, 3)
                    for pair in range(2):
                        act.wait_ge(s_hv, 2 * k + pair + 1)
                        if pair == 0:
                            wait_for(act, s_z, k)
                        nc.scalar.copy(vh[:, 2 * pair:2 * pair + 2, :].rearrange("p a b -> p (a b)"),
                                       bank[4 + pair][:, :]).then_inc(s_hv_sb, 1)
                if has(k, 1):
                    act.wait_ge(s_zneg, k)
                    nc.scalar.activation(zneg[:, :, :], zneg[:, :, :], ACT.Exp).then_inc(s_e, 1)
            act.wait_ge(s_wt_sb, 4)
            turns(act, body)

            act.wait_ge(s_gate, G * GATE_STEPS)
            nc.scalar.activation(wexp[:, :], gap[:, :], ACT.Exp).then_inc(s_gap, 1)

            def x_copy(t, u):
                act.wait_ge(s_tx, t + 1)
                wait_for(act, s_mm1, t - 1)
                nc.scalar.copy(xgT[:, u % 2, :], bank[u % 2][:, 0:P]).then_inc(s_xgt, 1)

            def ffn(k, last=False):
                no, regs = int_registers(act, expert_i, k * TU + BEFORE, TU, E - 1)
                for u in range(TU):
                    t = k * TU + u
                    act.wait_ge(s_mm1, t + 1)
                    wait_for(act, s_mm2, t - 3)
                    for c in range(FC):
                        r = nc.scalar.activation(hidT[:, u % 4, c * P:(c + 1) * P], bank[2 + u % 2][:, c * P:(c + 1) * P],
                                                 ACT.Relu, bias=b1_cols[:, bass.ds(no[u] * FC + c, 1)])
                    r.then_inc(s_hr, 1)
                    if not (last and u + 2 >= TU):
                        x_copy(t + 2, u)
                free_registers(act, regs)
            act.wait_ge(s_tab_done, 1)
            x_copy(0, 0)
            x_copy(1, 1)
            ffn(0)
            with act.Fori(1, TURNS - 1) as k:
                ffn(k)
            ffn(TURNS - 1, last=True)

        @block.tensor
        def _(pe):
            mm = nc.tensor.matmul
            pe.wait_ge(s_const, 1)
            pe.wait_ge(s_gnn_w, 16 * 9)
            nc.tensor.transpose(bank[0][:, 0:P], W_sb[:, :], ident[:, :])
            nc.tensor.transpose(bank[0][:, P:2 * P], a12_sb[:, :], ident[:, :])
            nc.tensor.transpose(bank[0][:, 2 * P:2 * P + E * FC], b1_rows[:, :], ident[0:E * FC, 0:E * FC]).then_inc(s_wt, 1)
            pe.wait_ge(s_wt_sb, 3)
            mm(bank[1][:, 0:D], a12T[:, :], WT[:, :], start=True, stop=True)
            mm(bank[1][:, D:D + 1], WT[:, :], a1_sb[:, :], start=True, stop=True)
            mm(bank[1][:, D + 1:D + 2], WT[:, :], a2_sb[:, :], start=True, stop=True).then_inc(s_wt, 1)
            pe.wait_ge(s_wt_sb, 6)
            mm(bank[2][:, 0:D], WT[:, :], C_sb[:, :], start=True, stop=True).then_inc(s_wt, 1)
            pe.wait_ge(s_wt_sb, 7)

            def prob_transposes(k, i):
                n = (k - 1) * TPG + i
                pe.wait_ge(s_exp, n + 1)
                wait_for(pe, s_ptd if i % 2 else s_pta, (k - 1) * 2 + i // 2)
                for c in range(TPG):
                    last = nc.tensor.transpose(bank[2 + i % 2][:, c * P:(c + 1) * P], prob[:, i, c * P:(c + 1) * P],
                                               ident[:, :])
                last.then_inc(s_pt, 1)

            def scores(k, i):
                if i == 0:
                    pe.wait_ge(s_mask, k + 1)
                    pe.wait_ge(s_qt_sb, k + 1)
                wait_for(pe, s_em, k * TPG + i - 1)
                mm(bank[i % 2][:, :], ident_bf[:, :], no_edge[:, i, :], start=True, stop=False)
                mm(bank[i % 2][:, :], qT[:, i * P:(i + 1) * P], featT[:, :], start=False, stop=True).then_inc(s_s, 1)

            def values(k, i):
                if i == 0:
                    wait_for(pe, s_z, k - 1)
                    pe.wait_ge(s_hv_sb, 2 * k)
                pe.wait_ge(s_ptd if i % 2 else s_pta, (k - 1) * 2 + i // 2 + 1)
                for c in range(TPG):
                    last = mm(bank[6][:, i * P:(i + 1) * P], probT[:, i % 2, c * P:(c + 1) * P], vh[:, c, 0:D],
                              start=(c == 0), stop=(c == TPG - 1))
                last.then_inc(s_pv, 1)

            def body(k):
                if has(k, 0):
                    pe.wait_ge(s_feat, k + 1)
                    wait_for(pe, s_hv_sb, 2 * k - 1)
                    for i in range(TPG):
                        last = nc.tensor.transpose(bank[4][:, i * P:(i + 1) * P], feat[:, i, :], ident[:, :])
                    last.then_inc(s_ft, 1)
                if has(k, 3):
                    pe.wait_ge(s_member, k - 2)
                    for a in range(TPG + 1):
                        o = bank[7][:, E * (a + 1):E * (a + 2)]
                        for c in range(a):
                            last = mm(o, ones_bf[:, :], member[:, c, :], start=(c == 0), stop=(a == TPG and c == a - 1))
                        if a < TPG:
                            last = mm(o, before_bf[:, :], member[:, a, :], start=(a == 0), stop=True)
                    last.then_inc(s_rank, 1)
                if has(k, 0):
                    pe.wait_ge(s_ft_sb, k + 1)
                    wait_for(pe, s_hv_sb, 2 * k)
                    mm(bank[5][:, :], M_sb[:, :], featT[:, :], start=True, stop=True).then_inc(s_qt, 1)
                    wait_for(pe, s_member, k - 2)
                    wait_for(pe, s_slot, k - 2)
                    wait_for(pe, s_ay, k)
                    for i in range(TPG):
                        last = mm(bank[7][:, i:i + 1], featT[:, i * P:(i + 1) * P], u2[:, :], start=True, stop=True)
                    last.then_inc(s_small, 1)
                for i in range(TPG):
                    if has(k, 1):
                        prob_transposes(k, i)
                    if has(k, 0):
                        scores(k, i)
                    if i == 2 and has(k, 2):
                        pe.wait_ge(s_x2t_sb, k - 1)
                        for c in range(TPG):
                            last = mm(bank[7][:, E * (c + 1):E * (c + 2)], x2T[:, c * P:(c + 1) * P], gate_sb[:, :],
                                      start=True, stop=True)
                        last.then_inc(s_logit, 1)
                    if has(k, 1):
                        values(k, i)
                    if i == 1 and has(k, 2):
                        pe.wait_ge(s_x2n, k - 1)
                        pe.wait_ge(s_ay, min(k + 1, G) if isinstance(k, int) else k + 1)
                        wait_for(pe, s_slot, k - 2)
                        for c in range(TPG):
                            last = nc.tensor.transpose(bank[7][:, c * P:(c + 1) * P], row[:, c, 0:D], ident[:, :])
                        last.then_inc(s_x2t, 1)
                if has(k, 0):
                    for i in range(TPG):
                        last = mm(bank[4 + i // 2][:, (i % 2) * 2 * D:(i % 2 + 1) * 2 * D], featT[:, i * P:(i + 1) * P],
                                  W21[:, :], start=True, stop=True)
                        if i % 2:
                            last.then_inc(s_hv, 1)
            turns(pe, body)

            pe.wait_ge(s_late, 16 * 5)
            pe.wait_ge(s_tab_done, 1)

            def x_transpose(t, k, u):
                pe.wait_ge(s_xg[u], 16 * (k + 1))
                nc.tensor.transpose(bank[u % 2][:, 0:P], xg[:, u, 0:D], ident[:, :]).then_inc(s_tx, 1)

            def ffn(k, first=False, last=False):
                no, regs = int_registers(pe, expert_i, k * TU, TU + BEFORE, E - 1)
                for u in range(TU):
                    t = k * TU + u
                    pe.wait_ge(s_xgt, t + 1)
                    pe.wait_ge(s_wc, t + 1)
                    wait_for(pe, s_hr, t - 1)
                    for c in range(FC):
                        m1 = mm(bank[2 + u % 2][:, c * P:(c + 1) * P], w1_cur[:, u % 4, c * P:(c + 1) * P],
                                xgT[:, u % 2, :], start=True, stop=True)
                    m1.then_inc(s_mm1, 1)
                    if not (first and u < BEFORE):
                        second(t - BEFORE, (u - BEFORE) % 4, no[u])
                    if not (last and u + 2 >= TU):
                        if u + 2 < TU:
                            x_transpose(t + 2, k, u + 2)
                        else:
                            x_transpose(t + 2, k + 1, u + 2 - TU)
                if last:
                    for u in range(BEFORE):
                        second(TURNS * TU - BEFORE + u, (TU - BEFORE + u) % 4, no[TU + u])
                free_registers(pe, regs)

            def second(t, b, e):
                pe.wait_ge(s_hr, t + 1)
                wait_for(pe, s_y, t - 1)
                for c in range(FC):
                    m2 = mm(bank[6 + b % 2][:, 0:D], hidT[:, b, c * P:(c + 1) * P],
                            w2_sb[:, bass.ds((e * FC + c) * D, D)], start=(c == 0), stop=(c == FC - 1))
                m2.then_inc(s_mm2, 1)

            x_transpose(0, 0, 0)
            x_transpose(1, 0, 1)
            ffn(0, first=True)
            with pe.Fori(1, TURNS - 1) as k:
                ffn(k)
            ffn(TURNS - 1, last=True)

        @block.vector
        def _(dve):
            V = nc.vector
            setup = Steps(dve, s_wt_sb, 0, 7)
            dve.wait_ge(s_wt, 1)
            setup.did(V.tensor_copy(WT[:, :], bank[0][:, 0:P]))
            setup.did(V.tensor_copy(a12T[:, :], bank[0][:, P:2 * P]))
            setup.did(V.tensor_copy(b1_cols[:, :], bank[0][:, 2 * P:2 * P + E * FC]))
            dve.wait_ge(s_wt, 2)
            setup.did(V.tensor_copy(u1[:, :], bank[1][:, D:D + 1]))
            setup.did(V.tensor_copy(u2[:, :], bank[1][:, D + 1:D + 2]))
            setup.did(V.tensor_copy(C_sb[:, :], bank[1][:, 0:D]))
            dve.wait_ge(s_wt, 3)
            setup.did(V.tensor_copy(M_sb[:, :], bank[2][:, 0:D]))

            def xt(k, i):
                t = k * TPG + i
                return x_sb[:, t, :] if isinstance(t, int) else x_sb[:, bass.ds(t, 1), :].rearrange("p a d -> p (a d)")

            def xg_of(k):
                return x_sb[:, k * TPG:(k + 1) * TPG, :] if isinstance(k, int) else x_sb[:, bass.ds(k * TPG, TPG), :]

            def mask(k):
                dve.wait_ge(s_adj, 16 * (k + 1))
                wait_for(dve, s_s, k * TPG)
                V.tensor_scalar(no_edge[:, :, :], adj_sb[:, :, :], 0.0, NEG_INF, ALU.is_le, ALU.mult).then_inc(s_mask, 1)

            def stats(k, o, s_stats, s_made):
                settle(dve)
                for i in range(TPG):
                    last = V.bn_stats(bn[:, o + i, :], xt(k, i))
                last.then_inc(s_stats, 1)
                dve.wait_ge(s_stats, k + 1)
                settle(dve)
                for i in range(TPG):
                    last = V.bn_aggr(mv[:, o + i, :], bn[:, o + i, :])
                last.then_inc(s_made, 1)

            V.memset(mv[:, :, :], 1.0).then_inc(s_bn, 1)
            dve.wait_ge(s_bn, 1)
            dve.wait_ge(s_x, 16)
            stats(0, 0, s_bn1, s_mv1)
            mask(0)
            dve.wait_ge(s_rs1, 1)
            for i in range(TPG):
                ins = V.tensor_scalar(feat[:, i, :], xt(0, i), mv[:, i, 0:1], rstd[:, i:i + 1], ALU.subtract, ALU.mult)
            ins.then_inc(s_feat, 1)

            def body(k):
                if has(k, 3):
                    slot(k - 3)
                if has(k, 0):
                    dve.wait_ge(s_small, k + 1)
                    V.tensor_scalar(tiles_of(ay4, k), bank[7][:, 0:TPG], 4.0, None, ALU.mult).then_inc(s_ay, 1)
                for i in range(TPG):
                    if has(k, 0):
                        dve.wait_ge(s_relu, k * TPG + i + 1)
                        wait_for(dve, s_pt, (k - 1) * TPG + i + 1)
                        settle(dve)
                        V.tensor_tensor_reduce(prob[:, i, :], bank[i % 2][:, :], relu4[:, i % 2, :], -ALPHA, 3e38,
                                               ALU.add, ALU.min, row_min[:, i:i + 1]).then_inc(s_em, 1)
                    if has(k, 1) and i % 2 == 0:
                        n = (k - 1) * TPG + i + 1
                        dve.wait_ge(s_pt, n + 1)
                        wait_for(dve, s_pv, n - 1)
                        V.tensor_copy(probT[:, 1, :], bank[3][:, :]).then_inc(s_ptd, 1)
                    if i == 0 and has(k, -1):
                        dve.wait_ge(s_x, 16 * (k + 2))
                        stats(k + 1, 0, s_bn1, s_mv1)
                    if i == 2 and has(k, -1):
                        dve.wait_ge(s_rs1, k + 2)
                        dve.wait_ge(s_ft, k + 1)
                        for c in range(TPG):
                            last = V.tensor_scalar(feat[:, c, :], xt(k + 1, c), mv[:, c, 0:1], rstd[:, c:c + 1],
                                                   ALU.subtract, ALU.mult)
                        last.then_inc(s_feat, 1)
                    if i == 2 and has(k, 2):
                        gate(k - 2)
                if has(k, 1):
                    zs = Steps(dve, s_zs, k - 1, 3)
                    dve.wait_ge(s_exp, k * TPG)
                    zs.did(V.reciprocal(rinv[:, :], tiles_of(row_sum, k - 1)))
                    zs.wait()
                    dve.wait_ge(s_pv, k * TPG)
                    for i in range(TPG):
                        last = V.scalar_tensor_tensor(out=z[:, i, :], in0=bank[6][:, i * P:(i + 1) * P],
                                                      scalar=rinv[:, i:i + 1], in1=vh[:, i, D:2 * D], op0=ALU.mult,
                                                      op1=ALU.add)
                    last.then_inc(s_z, 1)
                    dve.wait_ge(s_z, k)
                    V.tensor_scalar(zneg[:, :, :], z[:, :, :], 0.0, None, ALU.min).then_inc(s_zneg, 1)
                    zs.did(V.scalar_tensor_tensor(out=z[:, :, :], in0=z[:, :, :], scalar=0.0, in1=xg_of(k - 1),
                                                  op0=ALU.max, op1=ALU.add))
                if has(k, -1):
                    mask(k + 1)
                if has(k, 1):
                    dve.wait_ge(s_e, k)
                    zs.wait()
                    zs.did(V.scalar_tensor_tensor(out=xg_of(k - 1), in0=zneg[:, :, :], scalar=-1.0, in1=z[:, :, :],
                                                  op0=ALU.add, op1=ALU.add))
                    zs.wait()
                    zs.end()
                    stats(k - 1, TPG, s_bn2, s_mv2)
                    dve.wait_ge(s_rs2, k)
                    wait_for(dve, s_row_out, k - 1)
                    wait_for(dve, s_row_kept, k - 1)
                    for i in range(TPG):
                        last = V.tensor_scalar(row[:, i, 0:D], xt(k - 1, i), mv[:, TPG + i, 0:1],
                                               rstd[:, TPG + i:TPG + i + 1], ALU.subtract, ALU.mult)
                    last.then_inc(s_x2n, 1)

            def gate(g):
                s = Steps(dve, s_gate, g, GATE_STEPS)
                dve.wait_ge(s_logit, g + 1)
                s.did(V.tensor_tensor(logit[:, :, :], bank[7][:, E:E + TPG * E].rearrange("p (a e) -> p a e", a=TPG),
                                      gate_bias[:, :].rearrange("p (a e) -> p a e", a=1).to_broadcast((P, TPG, E)), ALU.add))
                s.wait()
                settle(dve)
                for i in range(TPG):
                    last = V.max(top[:, i, :], logit[:, i, :])
                s.did(last)
                s.wait()
                settle(dve)
                for i in range(TPG):
                    V.max_index(top_no[:, i, :], top[:, i, :], logit[:, i, :])
                s.did(V.tensor_tensor(tiles_of(gap, g), top[:, :, 1:2].rearrange("p a b -> p (a b)"),
                                      top[:, :, 0:1].rearrange("p a b -> p (a b)"), ALU.subtract))
                s.wait()
                s.did(V.tensor_copy(chosen[:, :, :], top_no[:, :, 0:K]))
                s.wait()
                V.tensor_copy(row[:, :, D:D + 1].rearrange("p a b -> p (a b)"), tiles_of(token2, g))
                V.tensor_copy(row[:, :, D + 1:D + 2], chosen[:, :, 0:1])
                s.did(V.tensor_tensor(onehot[:, :, :],
                                      expert_no[:, :].rearrange("p (a e) -> p a e", a=1).to_broadcast((P, TPG * K, E)),
                                      chosen[:, :, :].rearrange("p a b -> p (a b)").rearrange("p (a b) -> p a b", b=1).to_broadcast((P, TPG * K, E)),
                                      ALU.is_equal))
                s.wait()
                oh = onehot[:, :, :].rearrange("p (a k) e -> p a k e", k=K)
                V.tensor_tensor(member[:, :, :], oh[:, :, 0, :], oh[:, :, 1, :], ALU.add).then_inc(s_member, 1)
                s.end()

            def slot(g):
                s = Steps(dve, s_slots, g, SLOT_STEPS)
                dve.wait_ge(s_rank, g + 1)
                s.did(V.tensor_tensor(place[:, :, :], bank[7][:, E:(TPG + 1) * E].rearrange("p (a e) -> p a e", a=TPG),
                                      base[:, :].rearrange("p (a e) -> p a e", a=1).to_broadcast((P, TPG, E)), ALU.add))
                s.wait()
                for j in range(K):
                    V.tensor_tensor(picked[:, :, :].rearrange("p (a k) e -> p a k e", k=K)[:, :, j, :],
                                          onehot[:, :, :].rearrange("p (a k) e -> p a k e", k=K)[:, :, j, :],
                                          place[:, :, :], ALU.mult)
                s.did(V.tensor_tensor(base[:, :], base[:, :], bank[7][:, (TPG + 1) * E:(TPG + 2) * E], ALU.add))
                s.wait()
                bin_wait(dve, g)
                with nc.allow_low_precision(reason="summed in float32; row numbers are whole"):
                    V.tensor_reduce(slots[:, :, :].rearrange("p a k -> p (a k)"), picked[:, :, :], AX_X,
                                    ALU.add).then_inc(s_slot, 1)
                s.end()

            dve.wait_ge(s_const, 1)
            turns(dve, body)

            tb = Steps(dve, s_tab, 0, 999)
            dve.wait_ge(s_slots, G * SLOT_STEPS)
            tb.did(V.tensor_copy(base_i[:, :], base[:, :]))
            tb.did(V.tensor_tensor(cnt[:, :], base[:, :], bin_start[:, :], ALU.subtract))
            tb.wait()
            tb.did(V.tensor_scalar(cnt_i[:, :], cnt[:, :], float(P - 1), None, ALU.add))
            tb.did(V.memset(scan[0][:, :], 0.0))
            tb.did(V.memset(scan[1][:, :], 0.0))
            tb.wait()
            tb.did(V.tensor_scalar(ntile_i[:, :], cnt_i[:, :], 7, None, ALU.logical_shift_right))
            tb.wait()
            tb.did(V.tensor_copy(scan[0][:, PADC:], ntile_i[:, :]))
            for n, by in enumerate((1, 2, 4, 8)):
                tb.wait()
                a, b = scan[n % 2], scan[1 - n % 2]
                tb.did(V.tensor_tensor(b[:, PADC:], a[:, PADC:], a[:, PADC - by:PADC + E - by], ALU.add))
            tb.wait()
            ends = scan[0][:, PADC:].rearrange("p (a e) -> p a e", a=1).to_broadcast((P, XT, E))
            tb.did(V.tensor_tensor(passed[:, :, :], ends,
                                   tile_no[:, :].rearrange("p (a e) -> p a e", e=1).to_broadcast((P, XT, E)), ALU.is_le))
            tb.wait()
            tb.did(V.tensor_reduce(expert_of[:, :], passed[:, :, :], AX_X, ALU.add))
            tb.wait()
            tb.did(V.tensor_tensor(passed[:, :, :], passed[:, :, :], ends, ALU.mult))
            tb.wait()
            tb.did(V.tensor_reduce(start_of[:, :], passed[:, :, :], AX_X, ALU.max))
            tb.did(V.tensor_scalar(expert_w[:, :], expert_of[:, :], float(E - 1), None, ALU.min))
            tb.did(V.tensor_scalar(first_row[:, :], expert_of[:, :], float(BIN), None, ALU.mult))
            tb.did(V.memset(expert_i[:, 0:BEFORE], 0))
            tb.did(V.memset(expert_i[:, BEFORE + XT:], 0))
            tb.wait()
            tb.did(V.tensor_copy(expert_i[:, BEFORE:BEFORE + XT], expert_w[:, :]))
            tb.did(V.tensor_tensor(start_of[:, :], tile_no[:, :], start_of[:, :], ALU.subtract))
            tb.wait()
            tb.did(V.scalar_tensor_tensor(out=first_row[:, :], in0=start_of[:, :], scalar=float(P), in1=first_row[:, :],
                                          op0=ALU.mult, op1=ALU.add))
            tb.wait()
            V.tensor_scalar(first_row_i[:, :], first_row[:, :], float(PAD_ROW), None, ALU.min).then_inc(s_tab_done, 1)

            dve.wait_ge(s_late, 16 * 5)
            dve.wait_ge(s_tab_done, 1)

            def out_of(t, u, e, tn):
                dve.wait_ge(s_mm2, t + 1)
                wait_for(dve, s_sc[u], 16 * tn)
                V.scalar_tensor_tensor(out=dest[:, u:u + 1], in0=xg[:, u, D + 1:D + 2],
                                       scalar=expert_of[:, t:t + 1] if isinstance(t, int) else expert_of[:, bass.ds(t, 1)],
                                       in1=xg[:, u, D:D + 1], op0=ALU.not_equal, op1=ALU.add)
                V.tensor_tensor(y[:, u, :], bank[6 + u % 2][:, 0:D], b2_all[:, bass.ds(e * D, D)], ALU.add).then_inc(s_y, 1)

            def w1_copy(t, u, e):
                wait_for(dve, s_mm1, t - 3)
                V.tensor_copy(w1_cur[:, u % 4, :], w1_sb[:, bass.ds(e * F, F)]).then_inc(s_wc, 1)

            def ffn(k, first=False, last=False):
                no, regs = int_registers(dve, expert_i, k * TU, BEFORE + TU + 1, E - 1)
                for u in range(TU):
                    t = k * TU + u
                    if first and u == 0:
                        w1_copy(0, 0, no[BEFORE])
                    if not (last and u == TU - 1):
                        w1_copy(t + 1, u + 1, no[BEFORE + u + 1])
                    if u >= BEFORE:
                        out_of(t - BEFORE, u - BEFORE, no[u], k)
                    elif not first:
                        out_of(t - BEFORE, TU - BEFORE + u, no[u], k - 1)
                if last:
                    for u in range(BEFORE):
                        out_of(TURNS * TU - BEFORE + u, TU - BEFORE + u, no[TU + u], TURNS - 1)
                free_registers(dve, regs)
            ffn(0, first=True)
            ffn(1)
            with dve.Fori(2, TURNS - 1) as k:
                ffn(k)
            ffn(TURNS - 1, last=True)

            dve.wait_ge(s_gap, 1)
            V.tensor_scalar(wsum[:, :], wexp[:, :], 1.0, None, ALU.add).then_inc(s_w, 1)
            dve.wait_ge(s_w, 1)
            V.reciprocal(wt[:, 0, :], wsum[:, :]).then_inc(s_w, 1)
            dve.wait_ge(s_w, 2)
            V.tensor_tensor(wt[:, 1, :], wexp[:, :], wt[:, 0, :], ALU.mult).then_inc(s_w, 1)
            dve.wait_ge(s_w, 3)

            def final(h, b):
                g = 2 * h + b
                s = Steps(dve, s_fin, g, 4 * TPG + 2)
                dve.wait_ge(s_yy[b], 16 * (h + 1))
                for j in range(K):
                    if j:
                        s.wait()
                    for i in range(TPG):
                        t = g * TPG + i
                        wc = wt[:, j, t:t + 1] if isinstance(t, int) else wt[:, j, bass.ds(t, 1)]
                        prev = acc[:, 0, i, :] if j else (xn_all[:, t, :] if isinstance(t, int) else xn_all[:, bass.ds(t, 1), :].rearrange("p a d -> p (a d)"))
                        ins = V.scalar_tensor_tensor(out=acc[:, 0, i, :], in0=yy[:, b, i, j * D:(j + 1) * D], scalar=wc,
                                                     in1=prev, op0=ALU.mult, op1=ALU.add)
                        if j == K - 1 and i == TPG - 1:
                            ins.then_inc(s_fn, 1)
                        elif j == 0:
                            s.did(ins)
                dve.wait_ge(s_fn, g + 1)
                settle(dve)
                for i in range(TPG):
                    s.did(V.bn_stats(bn[:, i, :], acc[:, 0, i, :]))
                s.wait()
                settle(dve)
                for i in range(TPG):
                    s.did(V.bn_aggr(mv[:, i, :], bn[:, i, :]))
                s.wait()
                V.memset(bn[:, 0, 0:1], 0.0).then_inc(s_fmv, 1)
                dve.wait_ge(s_frs, g + 1)
                for i in range(TPG):
                    s.did(V.tensor_scalar(acc[:, 0, i, :], acc[:, 0, i, :], mv[:, i, 0:1], rstd[:, i:i + 1], ALU.subtract, ALU.mult))
                s.wait()
                wait_for(dve, s_out[b], 16 * h)
                s.did(V.tensor_tensor(outn[:, b, :, :], acc[:, 0, :, :],
                                      gamma_all[:, :].rearrange("p (a d) -> p a d", a=1).to_broadcast((P, TPG, D)), ALU.mult))
                s.wait()
                s.did(V.tensor_tensor(outn[:, b, :, :], outn[:, b, :, :],
                                      beta_all[:, :].rearrange("p (a d) -> p a d", a=1).to_broadcast((P, TPG, D)), ALU.add))
                s.wait()
                V.tensor_tensor(outn[:, b, :, :], outn[:, b, :, :], xg_of(g), ALU.add).then_inc(s_fo, 1)
                s.end()
            for b in range(2):
                final(0, b)
            with dve.Fori(1, G // 2) as h:
                for b in range(2):
                    final(h, b)


_INS = ["x", "adj", "L0_gnn_W", "L0_gnn_a_1", "L0_gnn_a_2", "L0_gnn_a_12", "L0_gnn_W_1", "L0_gnn_W_2", "L0_ffn_gate_w",
        "L0_ffn_gate_b", "L0_ffn_w1", "L0_ffn_b1", "L0_ffn_w2", "L0_ffn_b2", "L0_ffn_gamma", "L0_ffn_beta"]


def kernel(**inputs):
    import numpy as _np
    import concourse.bacc as _bacc
    from concourse import mybir as _mybir
    from concourse.bass_utils import run_bass_kernel_spmd as _run

    nc = _bacc.Bacc("TRN2", target_bir_lowering=False, num_devices=1)
    arrays, args = {}, []
    for name in _INS:
        a = _np.ascontiguousarray(inputs[name])
        arrays[f"in_{name}_dram"] = a
        args.append(nc.dram_tensor(f"in_{name}_dram", a.shape, _mybir.dt.from_np(a.dtype), kind="ExternalInput").ap())
    out = nc.dram_tensor("out_0_dram", arrays["in_x_dram"].shape, _mybir.dt.float32, kind="ExternalOutput").ap()
    graph_attention_and_routed_experts(nc, *args, out)
    r = _run(nc, [arrays], core_ids=[0])
    return r.results[0]["out_0_dram"]
```

```python
from contextlib import ExitStack

import concourse.bass as bass
from concourse import mybir

F32 = mybir.dt.float32
BF16 = mybir.dt.bfloat16
I32 = mybir.dt.int32
U32 = mybir.dt.uint32
ALU = mybir.AluOpType
ACT = mybir.ActivationFunctionType
AX_X = mybir.AxisListType.X

P = 128
ALPHA = 0.2
NEG_INF = -9e15
EPS = 1e-5
FAR = float(1 << 20)


def graph_attention_and_routed_experts(nc, x, adj, W, a_1, a_2, a_12, W_1, W_2, gate_w, gate_b, w1, b1, w2, b2,
                                       gamma, beta, out):
    G, N, D = x.shape
    TPG = N // P
    TILES = G * TPG
    TOK = G * N
    E, _, F = w1.shape
    FC = F // P
    K = 2
    assert D == P and N == 512 and FC == 2 and E == 16

    META = 2
    ROW = D + META
    BIN = TOK + P
    PAD_ROW = E * BIN
    TU = 16
    XS = 8
    XR = TU // XS
    XT = TOK * K // P + E
    XC = 2
    XP = XT // XC
    assert XT % TU == 0
    TURNS = XT // TU
    assert 2 * (TURNS - 1) == G
    YB = 4
    AHEAD = 2
    BEFORE = 2

    bins = nc.dram_tensor("expert_bins", (PAD_ROW + P, ROW), F32, kind="Internal").ap()
    results = nc.dram_tensor("expert_results", (TOK * K, D), F32, kind="Internal").ap()

    with ExitStack() as ctx:
        def sb(name, shape, dt=F32):
            return ctx.enter_context(nc.sbuf_tensor(name, shape, dt))

        def sem(name):
            return ctx.enter_context(nc.semaphore(name))

        bank = [ctx.enter_context(nc.psum_tensor(f"bank{i}", [P, 512], F32)) for i in range(8)]

        ident = sb("ident", [P, P])
        ident_bf = sb("ident_bf", [P, P], BF16)
        ones_bf = sb("ones_bf", [P, P], BF16)
        before_bf = sb("before_bf", [P, P], BF16)
        expert_no = sb("expert_no", [P, E])
        bin_start = sb("bin_start", [P, E])
        tile_no = sb("tile_no", [P, XC])
        ones = sb("ones", [P, P])
        half = sb("half", [P, 2 * TPG])
        pad_rows = sb("pad_rows", [P, ROW])
        W_sb = sb("W_sb", [P, D])
        a12_sb = sb("a12_sb", [P, D])
        a1_sb = sb("a1_sb", [P, 1])
        a2_sb = sb("a2_sb", [P, 1])
        WT = sb("WT", [P, D])
        a12T = sb("a12T", [P, D])
        C_sb = sb("C_sb", [P, D])
        M_sb = sb("M_sb", [P, D])
        u1 = sb("u1", [P, 1])
        u2 = sb("u2", [P, 1])
        W21 = sb("W21", [P, 2 * D])
        gate_sb = sb("gate_sb", [P, E])
        gate_bias = sb("gate_bias", [P, E])
        w1_sb = sb("w1_sb", [P, E * F])
        w2_sb = sb("w2_sb", [P, E * FC * D])
        b1_rows = sb("b1_rows", [E * FC, P])
        b1_cols = sb("b1_cols", [P, E * FC])
        b2_all = sb("b2_all", [P, E * D])
        gamma_all = sb("gamma_all", [P, D])
        beta_all = sb("beta_all", [P, D])

        x_sb = sb("x_sb", [P, TILES, D])
        token2 = sb("token2", [P, TILES])
        ay4 = sb("ay4", [P, TILES])
        row_min = sb("row_min", [P, TPG])
        row_sum = sb("row_sum", [P, TILES])
        gap = sb("gap", [P, TPG])
        gate_exp = sb("gate_exp", [P, TPG])
        gate_sum = sb("gate_sum", [P, TPG])

        with ExitStack() as graph_only:
            adj_sb = graph_only.enter_context(nc.sbuf_tensor("adj_sb", [P, TPG, N], I32))
            no_edge = graph_only.enter_context(nc.sbuf_tensor("no_edge", [P, TPG, N], BF16))
            relu4 = graph_only.enter_context(nc.sbuf_tensor("relu4", [P, 2, N], F32))
            prob = graph_only.enter_context(nc.sbuf_tensor("prob", [P, TPG, N], F32))
        yy = sb("yy", [P, YB, TPG, K * D])
        outn = sb("outn", [P, YB, TPG, D])
        feat = sb("feat", [P, TPG, D])
        featT = sb("featT", [P, 2, N])
        qT = sb("qT", [P, 2, N])
        vh = sb("vh", [P, 2, TPG, 2 * D])
        probT = sb("probT", [P, 2, N])
        z = sb("z", [P, TPG, D])
        zneg = sb("zneg", [P, TPG, D])
        rinv = sb("rinv", [P, TPG])
        bn = sb("bn", [P, 2 * TPG, 6])
        mv = sb("mv", [P, 2 * TPG, 2])
        var_eps = sb("var_eps", [P, 2 * TPG])
        rstd = sb("rstd", [P, 2 * TPG])
        row = sb("row", [P, TPG, D])
        row_out = sb("row_out", [P, 2, K, TPG, ROW])
        slots = sb("slots", [P, 2, TPG, K], U32)
        x2T = sb("x2T", [P, N])
        logit = sb("logit", [P, TPG, E])
        top = sb("top", [P, TPG, 8])
        top_no = sb("top_no", [P, TPG, 8], U32)
        chosen = sb("chosen", [P, TPG, K])
        onehot = sb("onehot", [P, TPG * K, E])
        member = sb("member", [P, TPG, E], BF16)
        base = sb("base", [P, E])
        place = sb("place", [P, TPG, E])
        picked = sb("picked", [P, TPG * K, E])

        base_i = sb("base_i", [P, E], I32)
        cnt = sb("cnt", [P, E])
        cnt_i = sb("cnt_i", [P, E], I32)
        ntile_i = sb("ntile_i", [P, E], I32)
        PADC = 8
        scan = [sb(f"scan{i}", [P, PADC + E]) for i in range(2)]
        passed = sb("passed", [P, XC, E])
        passed_ends = sb("passed_ends", [P, XC, E])
        col = sb("col", [P, 4, XC])
        diag = sb("diag", [P, 2, XT])
        first_row_i = sb("first_row_i", [P, XT], I32)
        expert_i = sb("expert_i", [P, BEFORE + XT + AHEAD], I32)

        xg = sb("xg", [P, XS, ROW])
        xgT = sb("xgT", [P, 2, P])
        w1_cur = sb("w1_cur", [P, 4, F])
        hidT = sb("hidT", [P, 4, F])
        y = sb("y", [P, XS, D])
        dest = sb("dest", [P, XS], U32)

        shift = sb("shift", [P, 2 * TPG])

        s_early, s_gnn_w, s_late, s_const = sem("early_loaded"), sem("gnn_weights_loaded"), sem("late_loaded"), sem("constants_made")
        s_wt, s_wt_sb = sem("setup_matmul_done"), sem("setup_copied")
        s_x, s_adj = sem("x_loaded"), sem("adj_loaded")
        s_mask = sem("mask_made")
        s_bn, s_bn1, s_bn2 = sem("first_stats_made"), sem("feat_stats_made"), sem("row_stats_made")
        s_mv1, s_mv2 = sem("feat_variances_made"), sem("row_variances_made")
        s_rs1, s_rs2 = sem("feat_rstd_made"), sem("row_rstd_made")
        s_row_out, s_row_kept, s_slots = sem("row_out_copied"), sem("row_kept"), sem("slot_steps")
        s_pow = [sem("feat_rstd_step"), sem("row_rstd_step")]
        s_feat, s_x2n = sem("feat_made"), sem("rows_made")
        s_ft, s_ft_sb = sem("featT_done"), sem("featT_copied")
        s_qt, s_qt_sb = sem("qT_done"), sem("qT_copied")
        s_small, s_ay, s_logit = sem("ay_done"), sem("ay_copied"), sem("logits_done")
        s_hv, s_hv_sb = sem("vh_done"), sem("vh_copied")
        s_s, s_relu, s_em, s_exp = sem("scores_done"), sem("relu_made"), sem("masked_logits_made"), sem("prob_made")
        s_pt, s_pta, s_ptd = sem("probT_done"), sem("probT_even_copied"), sem("probT_odd_copied")
        s_pv, s_z, s_zneg, s_e = sem("pv_done"), sem("z_made"), sem("zneg_made"), sem("elu_exp_made")
        s_zs = sem("z_steps")
        s_x2t, s_x2t_sb = sem("x2T_done"), sem("x2T_copied")
        s_gate = sem("gate_steps")
        s_member, s_rank, s_slot = sem("member_made"), sem("rank_done"), sem("slots_made")
        s_bin = [sem(f"rows_in_bins_{b}") for b in range(2)]
        s_tab, s_tab_done, s_pad = sem("table_steps"), sem("table_made"), sem("padding_written")
        s_diag, s_spread = sem("table_diagonals_made"), sem("table_spread")
        s_padrow = sem("pad_tile_written")
        s_xg = [sem(f"tokens_loaded_{u}") for u in range(XS)]
        s_tx, s_xgt = sem("xgT_done"), sem("xgT_copied")
        s_wc, s_mm1, s_hr = sem("w1_copied"), sem("hidden_done"), sem("hidden_relu_made")
        s_mm2, s_y = sem("expert_out_done"), sem("expert_out_made")
        s_sc = [sem(f"results_scattered_{u}") for u in range(XS)]
        s_gap, s_gexp, s_biased = sem("gap_made"), sem("gate_exp_made"), sem("bias_added")
        s_yy = [sem(f"results_loaded_{u}") for u in range(YB)]
        s_sum, s_fs, s_beta = sem("tokens_summed"), sem("final_stats"), sem("beta_added")
        s_shift = sem("final_shift_made")
        s_fg, s_fmv, s_frs, s_fn, s_fo = sem("gamma_used"), sem("final_var"), sem("final_rstd"), sem("final_normed"), sem("final_made")
        s_out = sem("out_stored")

        s_settled = {name: sem(f"waited_{name}") for name in ("Pool", "DVE")}

        def wait_for(eng, s, value):
            if not isinstance(value, int) or value > 0:
                eng.wait_ge(s, value)

        def settle(eng):
            eng.sem_inc(s_settled[eng.engine.name], 1)

        def tiles_of(array, k):
            return array[:, k * TPG:(k + 1) * TPG] if isinstance(k, int) else array[:, bass.ds(k * TPG, TPG)]

        def xg_of(k):
            return x_sb[:, k * TPG:(k + 1) * TPG, :] if isinstance(k, int) else x_sb[:, bass.ds(k * TPG, TPG), :]

        res_v = results.rearrange("(g i p k) d -> g p i (k d)", g=G, p=P, k=K)

        def load_results(eng, g, b):
            src = res_v[g] if isinstance(g, int) else res_v[bass.ds(g, 1)].rearrange("a p i d -> p (a i) d")
            eng.dma_start(yy[:, b, :, :], src).then_inc(s_yy[b], 16)

        def last_turns(eng, body):
            for g in range(YB):
                body(g, g)
            with eng.Fori(1, G // YB - 1) as h:
                for b in range(YB):
                    body(h * YB + b, b)
            for g in range(G - YB, G + YB):
                body(g, g % YB)

        def tile_at(array, k, i):
            t = k * TPG + i
            return array[:, bass.ds(t, 1)] if not isinstance(t, int) else array[:, t:t + 1]

        class Steps:

            def __init__(self, eng, s, turn, each, done=0):
                self.eng, self.s, self.turn, self.each, self.n = eng, s, turn, each, done

            def did(self, ins):
                ins.then_inc(self.s, 1)
                self.n += 1

            def wait(self):
                self.eng.wait_ge(self.s, self.turn * self.each + self.n)

            def end(self):
                assert self.n == self.each, (self.n, self.each)

        def turns(eng, body):
            for k in range(-2, 4):
                body(k, k % 2, k // 2)
            with eng.Fori(2, G // 2 - 1) as h:
                for b in range(2):
                    body(h * 2 + b, b, h)
            for k in range(G - 2, G + 3):
                body(k, k % 2, k // 2)

        def has(k, back):
            return not isinstance(k, int) or 0 <= k - back < G

        named = [0]

        def int_registers(eng, table, at, n, high):
            named[0] += 1
            regs = [eng.alloc_register(f"{table.name}_{named[0]}_{i}") for i in range(n)]
            eng.reg_load(regs, table[0:1, bass.ds(at, n)] if not isinstance(at, int) else table[0:1, at:at + n])
            out = [nc.s_assert_within(eng.snap(r), 0, high, skip_runtime_bounds_check_because="made from counts")
                   for r in regs]
            return out, regs

        def free_registers(eng, regs):
            for r in regs:
                eng.free_register(r)

        GATE_STEPS, SLOT_STEPS = 4, 3

        def bin_wait(eng, b, n):
            if not isinstance(n, int) or n > 0:
                eng.wait_ge(s_bin[b], 16 * K * TPG * n)

        block = ctx.enter_context(nc.Block())

        @block.sync
        def _(sp):
            x_v = x.rearrange("g (i p) d -> g p i d", p=P)
            adj_v = adj.rearrange("g (i p) j -> g p i j", p=P)
            sp.dma_start(x_sb[:, 0:TPG, :], x_v[0]).then_inc(s_x, 16)
            sp.dma_start(adj_sb[:, :, :], adj_v[0]).then_inc(s_adj, 16)
            for g in range(1, 3):
                sp.wait_ge(s_x, 16 * g)
                sp.dma_start(x_sb[:, g * TPG:(g + 1) * TPG, :], x_v[g]).then_inc(s_x, 16)

            def load_adj(g):
                sp.wait_ge(s_mask, g)
                src = adj_v[g] if isinstance(g, int) else adj_v[bass.ds(g, 1)].rearrange("a p i j -> p (a i) j")
                sp.dma_start(adj_sb[:, :, :], src).then_inc(s_adj, 16)

            with sp.Fori(1, G - 2) as g:
                load_adj(g)
                sp.wait_ge(s_x, 16 * g + 32)
                sp.dma_start(x_sb[:, bass.ds((g + 2) * TPG, TPG), :],
                             x_v[bass.ds(g + 2, 1)].rearrange("a p i d -> p (a i) d")).then_inc(s_x, 16)
            for g in range(G - 2, G):
                load_adj(g)
            sp.wait_ge(s_const, 1)
            sp.dma_start(bins[PAD_ROW:PAD_ROW + P, :], pad_rows[:, :]).then_inc(s_padrow, 16)
            sp.wait_ge(s_padrow, 16)
            sp.wait_ge(s_tab, 1)
            for e0 in range(0, E, 8):
                at, regs = int_registers(sp, base_i, e0, 8, PAD_ROW)
                for e in range(8):
                    sp.dma_start(bins[bass.ds(at[e], P), :], pad_rows[:, :]).then_inc(s_pad, 16)
                free_registers(sp, regs)
            sp.wait_ge(s_pad, 16 * E)
            sp.wait_ge(s_tab_done, 1)
            for b in range(2):
                bin_wait(sp, b, G // 2)

            def loads(k):
                at, regs = int_registers(sp, first_row_i, k * TU, TU, PAD_ROW)
                for u in range(TU):
                    t = k * TU + u
                    wait_for(sp, s_tx, t - XS + 1)
                    wait_for(sp, s_y, t - XS + 1)
                    sp.dma_start(xg[:, u % XS, :], bins[bass.ds(at[u], P), :]).then_inc(s_xg[u % XS], 16)
                free_registers(sp, regs)

            loads(0)
            with sp.Fori(1, TURNS) as k:
                loads(k)
            for u in range(XS):
                sp.wait_ge(s_sc[u], 16 * TURNS * XR)
            out_v = out.rearrange("g (i p) d -> g p i d", p=P)

            def store(g):
                sp.wait_ge(s_fo, g + 1)
                dst = out_v[g] if isinstance(g, int) else out_v[bass.ds(g, 1)].rearrange("a p i d -> p (a i) d")
                sp.dma_start(dst, xg_of(g)).then_inc(s_out, 16)

            for g in range(YB):
                load_results(sp, g, g)
            with sp.Fori(0, G) as g:
                store(g)
            sp.wait_ge(s_out, 16 * G)

        @block.gpsimd
        def _(pool):
            nc.gpsimd.memset(ident[:, :], 0.0)
            nc.gpsimd.memset(before_bf[:, :], 1.0)
            nc.gpsimd.memset(ones_bf[:, :], 1.0)
            nc.gpsimd.memset(ones[:, :], 1.0)
            nc.gpsimd.memset(half[:, :], -0.5)
            nc.gpsimd.memset(pad_rows[:, :], 0.0).then_inc(s_early, 1)
            pool.wait_ge(s_early, 1)
            nc.gpsimd.memset(pad_rows[:, D:D + 1], FAR)
            nc.gpsimd.affine_select(ident[:, :], ident[:, :], [[-1, P]], ALU.not_equal, 1.0, base=0,
                                    channel_multiplier=1)
            nc.gpsimd.affine_select(before_bf[:, :], before_bf[:, :], [[1, P]], ALU.is_gt, 0.0, base=0,
                                    channel_multiplier=-1).then_inc(s_early, 1)
            pool.wait_ge(s_early, 2)
            nc.gpsimd.tensor_copy(ident_bf[:, :], ident[:, :])
            nc.gpsimd.iota(expert_no[:, :], [[1, E]], base=0, channel_multiplier=0,
                           allow_small_or_imprecise_dtypes=True)
            nc.gpsimd.iota(bin_start[:, :], [[BIN, E]], base=0, channel_multiplier=0,
                           allow_small_or_imprecise_dtypes=True)
            nc.gpsimd.iota(base[:, :], [[BIN, E]], base=0, channel_multiplier=0,
                           allow_small_or_imprecise_dtypes=True)
            nc.gpsimd.iota(tile_no[:, :], [[XP, XC]], base=0, channel_multiplier=1,
                           allow_small_or_imprecise_dtypes=True)
            nc.gpsimd.iota(token2[:, :], [[K * P, TILES]], base=0, channel_multiplier=K,
                           allow_small_or_imprecise_dtypes=True).then_inc(s_const, 1)

            def rstds(o, n, made, done):
                pool.wait_ge(made, n)
                settle(pool)
                nc.gpsimd.tensor_scalar(var_eps[:, o:o + TPG], mv[:, o:o + TPG, 1:2].rearrange("p a b -> p (a b)"), EPS,
                                        None, ALU.add).then_inc(s_pow[o // TPG], 1)
                pool.wait_ge(s_pow[o // TPG], n)
                nc.gpsimd.tensor_tensor(rstd[:, o:o + TPG], var_eps[:, o:o + TPG], half[:, o:o + TPG],
                                        ALU.pow).then_inc(done, 1)

            def scatter_rows(g, b):
                pool.wait_ge(s_slot, g + 1)
                pool.wait_ge(s_row_out, g + 1)
                settle(pool)
                for i in range(TPG):
                    for j in range(K):
                        nc.gpsimd.indirect_dma_start(bins, bass.IndirectOffsetOnAxis(ap=slots[:, b, i, j:j + 1], axis=0),
                                                     row_out[:, b, j, i, :], None).then_inc(s_bin[b], 16)

            def body(k, b, h):
                if has(k, -2):
                    rstds(0, k + 3, s_mv1, s_rs1)
                if has(k, 2):
                    rstds(TPG, k - 1, s_mv2, s_rs2)
                if has(k, 3):
                    scatter_rows(k - 3, 1 - b)
            turns(pool, body)

            def scatter_results(k):
                for u in range(TU):
                    pool.wait_ge(s_y, k * TU + u + 1)
                    settle(pool)
                    nc.gpsimd.indirect_dma_start(results, bass.IndirectOffsetOnAxis(ap=dest[:, u % XS:u % XS + 1], axis=0),
                                                 y[:, u % XS, :], None, bounds_check=TOK * K - 1,
                                                 oob_is_err=False).then_inc(s_sc[u % XS], 16)
            with pool.Fori(0, TURNS) as k:
                scatter_results(k)

            def final_rstd(g, o):
                pool.wait_ge(s_fmv, g + 1)
                wait_for(pool, s_fn, g - 1)
                settle(pool)
                nc.gpsimd.tensor_scalar(var_eps[:, o:o + TPG], mv[:, 0:TPG, 1:2].rearrange("p a b -> p (a b)"), K * K * EPS,
                                        None,
                                        ALU.add).then_inc(s_pow[0], 1)
                pool.wait_ge(s_pow[0], g + G + 1)
                nc.gpsimd.tensor_tensor(rstd[:, o:o + TPG], var_eps[:, o:o + TPG], half[:, 0:TPG], ALU.pow).then_inc(s_frs, 1)
            def last_stage(g, b):
                if has(g, 0):
                    final_rstd(g, b % 2 * TPG)
                if has(g, 2):
                    pool.wait_ge(s_fn, g - 1)
                    nc.gpsimd.tensor_tensor(outn[:, (b - 2) % YB, :, :], outn[:, (b - 2) % YB, :, :],
                                            gamma_all[:, :].rearrange("p (a d) -> p a d", a=1).to_broadcast((P, TPG, D)),
                                            ALU.mult).then_inc(s_fg, 1)
            pool.wait_ge(s_late, 16 * 5)
            last_turns(pool, last_stage)

        @block.scalar
        def _(act):
            def bcast(v, n):
                return v.rearrange("(a n) -> a n", a=1).to_broadcast((P, n))
            for dst, src in ((W_sb[:, :], W), (a12_sb[:, :], a_12), (a1_sb[:, :], a_1), (a2_sb[:, :], a_2),
                             (W21[:, 0:D], W_2), (W21[:, D:2 * D], W_1), (gate_sb[:, :], gate_w),
                             (b1_rows[:, :], b1.rearrange("e (c p) -> (e c) p", p=P)),
                             (gate_bias[:, :], bcast(gate_b, E))):
                act.dma_start(dst, src).then_inc(s_gnn_w, 16)
            act.dma_start(w1_sb[:, :].rearrange("p (e f) -> p e f", e=E), w1.rearrange("e p f -> p e f")).then_inc(s_late, 16)
            act.dma_start(w2_sb[:, :].rearrange("p (a d) -> p a d", d=D),
                          w2.rearrange("e (c p) d -> p (e c) d", p=P)).then_inc(s_late, 16)
            act.dma_start(b2_all[:, :], bcast(b2.rearrange("e d -> (e d)"), E * D)).then_inc(s_late, 16)
            act.dma_start(gamma_all[:, :], bcast(gamma, D)).then_inc(s_late, 16)
            act.dma_start(beta_all[:, :], bcast(beta, D)).then_inc(s_late, 16)
            act.preload_act_table(ACT.Exp)

            def pt_copy(g, i):
                n = g * TPG + i
                act.wait_ge(s_pt, n + 1)
                wait_for(act, s_pv, n - 1)
                nc.scalar.copy(probT[:, 0, :], bank[2][:, :]).then_inc(s_pta, 1)

            def relu(k, i):
                act.wait_ge(s_s, k * TPG + i + 1)
                if i == 0:
                    act.wait_ge(s_ay, k + 1)
                nc.scalar.activation(relu4[:, i % 2, :], bank[i % 2][:, :], ACT.Relu, bias=tile_at(ay4, k, i),
                                     scale=4.0).then_inc(s_relu, 1)

            def exps(k, i):
                act.wait_ge(s_em, k * TPG + i + 1)
                nc.scalar.activation(prob[:, i, :], prob[:, i, :], ACT.Exp, bias=row_min[:, i:i + 1], scale=-1.0,
                                     accum_out=tile_at(row_sum, k, i)).then_inc(s_exp, 1)

            def elu_exp(g):
                act.wait_ge(s_zneg, g + 1)
                nc.scalar.activation(zneg[:, :, :], zneg[:, :, :], ACT.Exp).then_inc(s_e, 1)

            def rows_copy(g):
                act.wait_ge(s_x2t, g + 1)
                nc.scalar.copy(x2T[:, :], bank[7][:, :]).then_inc(s_x2t_sb, 1)

            def products_copy(k, b):
                for pair in range(2):
                    act.wait_ge(s_hv, 2 * k + pair + 1)
                    if pair == 0:
                        wait_for(act, s_z, k - 1)
                    nc.scalar.copy(vh[:, b, 2 * pair:2 * pair + 2, :].rearrange("p a b -> p (a b)"),
                                   bank[4 + pair][:, :]).then_inc(s_hv_sb, 1)

            def features_copy(g, b):
                act.wait_ge(s_ft, g + 1)
                nc.scalar.copy(featT[:, b, :], bank[4][:, :]).then_inc(s_ft_sb, 1)

            def queries_copy(g, b):
                act.wait_ge(s_qt, g + 1)
                nc.scalar.activation(qT[:, b, :], bank[5][:, :], ACT.Identity, bias=u1[:, :]).then_inc(s_qt_sb, 1)

            def rows_out(g, b, before):
                act.wait_ge(s_x2n, g + 1)
                bin_wait(act, b, before)
                nc.scalar.copy(row_out[:, b, 0, :, 0:D], row[:, :, :])
                nc.scalar.copy(row_out[:, b, 1, :, 0:D], row[:, :, :]).then_inc(s_row_out, 1)

            def gate_exps(g):
                act.wait_ge(s_gap, g + 1)
                wait_for(act, s_slot, g)
                nc.scalar.activation(gate_exp[:, :], gap[:, :], ACT.Exp).then_inc(s_gexp, 1)

            def body(k, b, h):
                if has(k, 0):
                    relu(k, 0)
                if has(k, 1):
                    pt_copy(k - 1, 0)
                if has(k, 0):
                    relu(k, 1)
                    exps(k, 0)
                if has(k, 3):
                    rows_copy(k - 3)
                if has(k, 0):
                    products_copy(k, b)
                if has(k, 1):
                    pt_copy(k - 1, 2)
                if has(k, 2):
                    elu_exp(k - 2)
                if has(k, 0):
                    exps(k, 1)
                    relu(k, 2)
                if has(k, -1):
                    features_copy(k + 1, 1 - b)
                if has(k, 3):
                    rows_out(k - 3, 1 - b, h - 2 + b)
                    gate_exps(k - 3)
                if has(k, 0):
                    relu(k, 3)
                    exps(k, 3)
                if has(k, -1):
                    queries_copy(k + 1, 1 - b)
                if has(k, 0):
                    exps(k, 2)
            act.wait_ge(s_wt_sb, 4)
            turns(act, body)

            def x_copy(t, u):
                act.wait_ge(s_tx, t + 1)
                wait_for(act, s_mm1, t - 1)
                nc.scalar.copy(xgT[:, u % 2, :], bank[u % 2][:, 0:P]).then_inc(s_xgt, 1)

            def w1_copy(t, u, e):
                wait_for(act, s_mm1, t - 3)
                nc.scalar.copy(w1_cur[:, u % 4, :], w1_sb[:, bass.ds(e * F, F)]).then_inc(s_wc, 1)

            def ffn(k, first=False, last=False):
                no, regs = int_registers(act, expert_i, k * TU + BEFORE, TU + AHEAD, E - 1)
                if first:
                    w1_copy(0, 0, no[0])
                    w1_copy(1, 1, no[1])
                for u in range(TU):
                    t = k * TU + u
                    if not (last and u + AHEAD >= TU):
                        w1_copy(t + AHEAD, u + AHEAD, no[u + AHEAD])
                    act.wait_ge(s_mm1, t + 1)
                    wait_for(act, s_mm2, t - 3)
                    for c in range(FC):
                        r = nc.scalar.activation(hidT[:, u % 4, c * P:(c + 1) * P], bank[2 + u % 2][:, c * P:(c + 1) * P],
                                                 ACT.Relu, bias=b1_cols[:, bass.ds(no[u] * FC + c, 1)])
                    r.then_inc(s_hr, 1)
                    if not (last and u + 2 >= TU):
                        x_copy(t + 2, u)
                free_registers(act, regs)
            act.wait_ge(s_tab_done, 1)
            act.wait_ge(s_late, 16 * 5)
            x_copy(0, 0)
            x_copy(1, 1)
            ffn(0, first=True)
            with act.Fori(1, TURNS - 1) as k:
                ffn(k)
            ffn(TURNS - 1, last=True)

            def last_stage(g, b):
                if has(g, 1):
                    act.wait_ge(s_shift, g)
                    wait_for(act, s_fo, g - YB)
                    o = (b + 1) % 2 * TPG
                    for i in range(TPG):
                        r = nc.scalar.activation(outn[:, (b - 1) % YB, i, :], yy[:, (b - 1) % YB, i, 0:D],
                                                 ACT.Identity, bias=shift[:, o + i:o + i + 1], scale=rstd[:, o + i:o + i + 1])
                    r.then_inc(s_fn, 1)
                    if not isinstance(g, int) or g - 1 + YB < G:
                        act.wait_ge(s_fn, g)
                        load_results(act, g - 1 + YB, (b - 1) % YB)
            last_turns(act, last_stage)

        @block.tensor
        def _(pe):
            mm = nc.tensor.matmul
            pe.wait_ge(s_const, 1)
            pe.wait_ge(s_gnn_w, 16 * 9)
            nc.tensor.transpose(bank[0][:, 0:P], W_sb[:, :], ident[:, :])
            nc.tensor.transpose(bank[0][:, P:2 * P], a12_sb[:, :], ident[:, :])
            nc.tensor.transpose(bank[0][:, 2 * P:2 * P + E * FC], b1_rows[:, :], ident[0:E * FC, 0:E * FC]).then_inc(s_wt, 1)
            pe.wait_ge(s_wt_sb, 3)
            mm(bank[1][:, 0:D], a12T[:, :], WT[:, :], start=True, stop=True)
            mm(bank[1][:, D:D + 1], WT[:, :], a1_sb[:, :], start=True, stop=True)
            mm(bank[1][:, D + 1:D + 2], WT[:, :], a2_sb[:, :], start=True, stop=True).then_inc(s_wt, 1)
            pe.wait_ge(s_wt_sb, 6)
            mm(bank[2][:, 0:D], WT[:, :], C_sb[:, :], start=True, stop=True).then_inc(s_wt, 1)
            pe.wait_ge(s_wt_sb, 7)

            def prob_transposes(g, i):
                pe.wait_ge(s_exp, g * TPG + i + 1)
                wait_for(pe, s_ptd if i % 2 else s_pta, g * 2 + i // 2)
                for c in range(TPG):
                    last = nc.tensor.transpose(bank[2 + i % 2][:, c * P:(c + 1) * P], prob[:, i, c * P:(c + 1) * P],
                                               ident[:, :])
                last.then_inc(s_pt, 1)

            def scores(k, b, i):
                if i == 0:
                    pe.wait_ge(s_mask, k + 1)
                    pe.wait_ge(s_qt_sb, k + 1)
                wait_for(pe, s_em, k * TPG + i - 1)
                mm(bank[i % 2][:, :], ident_bf[:, :], no_edge[:, i, :], start=True, stop=False)
                mm(bank[i % 2][:, :], qT[:, b, i * P:(i + 1) * P], featT[:, b, :], start=False, stop=True).then_inc(s_s, 1)

            def values(g, b, i):
                if i == 0:
                    wait_for(pe, s_z, g)
                    pe.wait_ge(s_hv_sb, 2 * g + 2)
                pe.wait_ge(s_ptd if i % 2 else s_pta, g * 2 + i // 2 + 1)
                for c in range(TPG):
                    last = mm(bank[6][:, i * P:(i + 1) * P], probT[:, i % 2, c * P:(c + 1) * P], vh[:, b, c, 0:D],
                              start=(c == 0), stop=(c == TPG - 1))
                last.then_inc(s_pv, 1)

            def ranks(g):
                pe.wait_ge(s_member, g + 1)
                for a in range(TPG + 1):
                    o = bank[7][:, E * (a + 1):E * (a + 2)]
                    for c in range(a):
                        last = mm(o, ones_bf[:, :], member[:, c, :], start=(c == 0), stop=(a == TPG and c == a - 1))
                    if a < TPG:
                        last = mm(o, before_bf[:, :], member[:, a, :], start=(a == 0), stop=True)
                last.then_inc(s_rank, 1)

            def features_products(k, b):
                pe.wait_ge(s_ay, k + 1)
                for i in range(TPG):
                    last = mm(bank[4 + i // 2][:, (i % 2) * 2 * D:(i % 2 + 1) * 2 * D],
                              featT[:, b, i * P:(i + 1) * P], W21[:, :], start=True, stop=True)
                    if i % 2:
                        last.then_inc(s_hv, 1)

            def rows_transposes(g):
                pe.wait_ge(s_x2n, g + 1)
                wait_for(pe, s_slot, g)
                for c in range(TPG):
                    last = nc.tensor.transpose(bank[7][:, c * P:(c + 1) * P], row[:, c, :], ident[:, :])
                last.then_inc(s_x2t, 1)

            def logits(g):
                pe.wait_ge(s_x2t_sb, g + 1)
                for c in range(TPG):
                    last = mm(bank[7][:, E * (c + 1):E * (c + 2)], x2T[:, c * P:(c + 1) * P], gate_sb[:, :],
                              start=True, stop=True)
                last.then_inc(s_logit, 1)

            def features_transposes(g):
                pe.wait_ge(s_feat, g + 1)
                wait_for(pe, s_hv_sb, 2 * g - 1)
                for i in range(TPG):
                    last = nc.tensor.transpose(bank[4][:, i * P:(i + 1) * P], feat[:, i, :], ident[:, :])
                last.then_inc(s_ft, 1)

            def queries(g, b):
                pe.wait_ge(s_ft_sb, g + 1)
                wait_for(pe, s_hv_sb, 2 * g)
                mm(bank[5][:, :], M_sb[:, :], featT[:, b, :], start=True, stop=True).then_inc(s_qt, 1)

            def row_logits(g, b):
                pe.wait_ge(s_ft_sb, g + 1)
                for i in range(TPG):
                    last = mm(bank[4][:, i:i + 1], featT[:, b, i * P:(i + 1) * P], u2[:, :], start=True, stop=True)
                last.then_inc(s_small, 1)

            def body(k, b, h):
                if has(k, 1):
                    prob_transposes(k - 1, 0)
                if has(k, 0):
                    scores(k, b, 0)
                if has(k, 1):
                    prob_transposes(k - 1, 1)
                if has(k, 0):
                    scores(k, b, 1)
                if has(k, 3):
                    rows_transposes(k - 3)
                if has(k, 0):
                    features_products(k, b)
                if has(k, 3):
                    logits(k - 3)
                if has(k, 1):
                    prob_transposes(k - 1, 2)
                    prob_transposes(k - 1, 3)
                    values(k - 1, 1 - b, 0)
                if has(k, 0):
                    scores(k, b, 2)
                if has(k, -1):
                    features_transposes(k + 1)
                if has(k, 3):
                    ranks(k - 3)
                if has(k, 0):
                    scores(k, b, 3)
                if has(k, 1):
                    values(k - 1, 1 - b, 1)
                if has(k, -1):
                    queries(k + 1, 1 - b)
                    row_logits(k + 1, 1 - b)
                if has(k, 1):
                    values(k - 1, 1 - b, 2)
                    values(k - 1, 1 - b, 3)
            turns(pe, body)

            pe.wait_ge(s_diag, 1)
            for j in range(2):
                last = mm(bank[0][:, j * XT:(j + 1) * XT], ones[0:XP, :], diag[0:XP, j, :], start=True, stop=True)
            last.then_inc(s_spread, 1)

            pe.wait_ge(s_late, 16 * 5)
            pe.wait_ge(s_tab_done, 1)

            def x_transpose(t, k, u):
                pe.wait_ge(s_xg[u % XS], 16 * (k * XR + u // XS + 1))
                nc.tensor.transpose(bank[u % 2][:, 0:P], xg[:, u % XS, 0:D], ident[:, :]).then_inc(s_tx, 1)

            def ffn(k, first=False, last=False):
                no, regs = int_registers(pe, expert_i, k * TU, TU + BEFORE, E - 1)
                for u in range(TU):
                    t = k * TU + u
                    pe.wait_ge(s_xgt, t + 1)
                    pe.wait_ge(s_wc, t + 1)
                    wait_for(pe, s_hr, t - 1)
                    for c in range(FC):
                        m1 = mm(bank[2 + u % 2][:, c * P:(c + 1) * P], w1_cur[:, u % 4, c * P:(c + 1) * P],
                                xgT[:, u % 2, :], start=True, stop=True)
                    m1.then_inc(s_mm1, 1)
                    if not (first and u < BEFORE):
                        second(t - BEFORE, (u - BEFORE) % 4, no[u])
                    if not (last and u + 2 >= TU):
                        if u + 2 < TU:
                            x_transpose(t + 2, k, u + 2)
                        else:
                            x_transpose(t + 2, k + 1, u + 2 - TU)
                if last:
                    for u in range(BEFORE):
                        second(TURNS * TU - BEFORE + u, (TU - BEFORE + u) % 4, no[TU + u])
                free_registers(pe, regs)

            def second(t, b, e):
                pe.wait_ge(s_hr, t + 1)
                wait_for(pe, s_biased, t - 1)
                for c in range(FC):
                    m2 = mm(bank[6 + b % 2][:, 0:D], hidT[:, b, c * P:(c + 1) * P],
                            w2_sb[:, bass.ds((e * FC + c) * D, D)], start=(c == 0), stop=(c == FC - 1))
                m2.then_inc(s_mm2, 1)

            x_transpose(0, 0, 0)
            x_transpose(1, 0, 1)
            ffn(0, first=True)
            with pe.Fori(1, TURNS - 1) as k:
                ffn(k)
            ffn(TURNS - 1, last=True)

        @block.vector
        def _(dve):
            V = nc.vector
            setup = Steps(dve, s_wt_sb, 0, 7)
            dve.wait_ge(s_wt, 1)
            setup.did(V.tensor_copy(WT[:, :], bank[0][:, 0:P]))
            setup.did(V.tensor_copy(a12T[:, :], bank[0][:, P:2 * P]))
            setup.did(V.tensor_copy(b1_cols[:, :], bank[0][:, 2 * P:2 * P + E * FC]))
            dve.wait_ge(s_wt, 2)
            setup.did(V.tensor_copy(u1[:, :], bank[1][:, D:D + 1]))
            setup.did(V.tensor_copy(u2[:, :], bank[1][:, D + 1:D + 2]))
            setup.did(V.tensor_copy(C_sb[:, :], bank[1][:, 0:D]))
            dve.wait_ge(s_wt, 3)
            setup.did(V.tensor_copy(M_sb[:, :], bank[2][:, 0:D]))

            def xt(k, i):
                t = k * TPG + i
                return x_sb[:, t, :] if isinstance(t, int) else x_sb[:, bass.ds(t, 1), :].rearrange("p a d -> p (a d)")

            def mask(k):
                dve.wait_ge(s_adj, 16 * (k + 1))
                wait_for(dve, s_s, k * TPG)
                V.tensor_scalar(no_edge[:, :, :], adj_sb[:, :, :], 0.0, NEG_INF, ALU.is_le, ALU.mult).then_inc(s_mask, 1)

            def stats(k, o, s_stats, s_made):
                settle(dve)
                for i in range(TPG):
                    last = V.bn_stats(bn[:, o + i, :], xt(k, i))
                last.then_inc(s_stats, 1)
                dve.wait_ge(s_stats, k + 1)
                settle(dve)
                for i in range(TPG):
                    last = V.bn_aggr(mv[:, o + i, :], bn[:, o + i, :])
                last.then_inc(s_made, 1)

            V.memset(mv[:, :, :], 1.0).then_inc(s_bn, 1)
            dve.wait_ge(s_bn, 1)

            def scores(k, i):
                dve.wait_ge(s_relu, k * TPG + i + 1)
                wait_for(dve, s_pt, (k - 1) * TPG + i + 1)
                settle(dve)
                V.tensor_tensor_reduce(prob[:, i, :], bank[i % 2][:, :], relu4[:, i % 2, :], -ALPHA, 3e38,
                                       ALU.add, ALU.min, row_min[:, i:i + 1]).then_inc(s_em, 1)

            def pt_copy(g, i):
                n = g * TPG + i
                dve.wait_ge(s_pt, n + 1)
                wait_for(dve, s_pv, n - 1)
                V.tensor_copy(probT[:, 1, :], bank[3][:, :]).then_inc(s_ptd, 1)

            def elu_parts(g, b):
                zs = Steps(dve, s_zs, g, 3)
                dve.wait_ge(s_pv, (g + 1) * TPG)
                zs.did(V.reciprocal(rinv[:, :], tiles_of(row_sum, g)))
                zs.wait()
                for i in range(TPG):
                    last = V.scalar_tensor_tensor(out=z[:, i, :], in0=bank[6][:, i * P:(i + 1) * P],
                                                  scalar=rinv[:, i:i + 1], in1=vh[:, b, i, D:2 * D], op0=ALU.mult,
                                                  op1=ALU.add)
                last.then_inc(s_z, 1)
                dve.wait_ge(s_z, g + 1)
                V.tensor_scalar(zneg[:, :, :], z[:, :, :], 0.0, None, ALU.min).then_inc(s_zneg, 1)

            def elu_sum(g):
                zs = Steps(dve, s_zs, g, 3, 1)
                zs.did(V.scalar_tensor_tensor(out=z[:, :, :], in0=z[:, :, :], scalar=0.0, in1=xg_of(g),
                                              op0=ALU.max, op1=ALU.add))
                dve.wait_ge(s_e, g + 1)
                zs.wait()
                zs.did(V.scalar_tensor_tensor(out=xg_of(g), in0=zneg[:, :, :], scalar=-1.0, in1=z[:, :, :],
                                              op0=ALU.add, op1=ALU.add))
                zs.wait()
                zs.end()

            def features(g):
                dve.wait_ge(s_rs1, g + 1)
                wait_for(dve, s_ft, g)
                for c in range(TPG):
                    last = V.tensor_scalar(feat[:, c, :], xt(g, c), mv[:, c, 0:1], rstd[:, c:c + 1],
                                           ALU.subtract, ALU.mult)
                last.then_inc(s_feat, 1)

            def rows(g):
                dve.wait_ge(s_rs2, g + 1)
                wait_for(dve, s_row_out, g)
                wait_for(dve, s_x2t, g)
                for i in range(TPG):
                    last = V.tensor_scalar(row[:, i, :], xt(g, i), mv[:, TPG + i, 0:1],
                                           rstd[:, TPG + i:TPG + i + 1], ALU.subtract, ALU.mult)
                last.then_inc(s_x2n, 1)

            def ay_copy(g):
                dve.wait_ge(s_small, g + 1)
                V.tensor_scalar(tiles_of(ay4, g), bank[4][:, 0:TPG], 4.0, None, ALU.mult).then_inc(s_ay, 1)

            def first_stats(g):
                dve.wait_ge(s_x, 16 * (g + 1))
                stats(g, 0, s_bn1, s_mv1)

            def body(k, b, h):
                if has(k, 1):
                    pt_copy(k - 1, 1)
                if has(k, 0):
                    scores(k, 0)
                if has(k, 2):
                    elu_parts(k - 2, b)
                if has(k, 0):
                    scores(k, 1)
                if has(k, -2):
                    first_stats(k + 2)
                if has(k, 3):
                    gate(k - 3)
                if has(k, 2):
                    elu_sum(k - 2)
                    stats(k - 2, TPG, s_bn2, s_mv2)
                if has(k, 0):
                    scores(k, 2)
                    scores(k, 3)
                if has(k, 1):
                    pt_copy(k - 1, 3)
                if has(k, 3):
                    slot(k - 3, 1 - b, h - 2 + b)
                if has(k, -1):
                    mask(k + 1)
                    ay_copy(k + 1)
                if has(k, -2):
                    features(k + 2)
                if has(k, 2):
                    rows(k - 2)
            def gate(g):
                s = Steps(dve, s_gate, g, GATE_STEPS)
                dve.wait_ge(s_logit, g + 1)
                s.did(V.tensor_tensor(logit[:, :, :], bank[7][:, E:E + TPG * E].rearrange("p (a e) -> p a e", a=TPG),
                                      gate_bias[:, :].rearrange("p (a e) -> p a e", a=1).to_broadcast((P, TPG, E)), ALU.add))
                s.wait()
                settle(dve)
                for i in range(TPG):
                    last = V.max(top[:, i, :], logit[:, i, :])
                s.did(last)
                s.wait()
                settle(dve)
                for i in range(TPG):
                    V.max_index(top_no[:, i, :], top[:, i, :], logit[:, i, :])
                wait_for(dve, s_gexp, g)
                V.tensor_tensor(gap[:, :], top[:, :, 1:2].rearrange("p a b -> p (a b)"),
                                top[:, :, 0:1].rearrange("p a b -> p (a b)"), ALU.subtract).then_inc(s_gap, 1)
                dve.wait_ge(s_gap, g + 1)
                s.did(V.tensor_copy(chosen[:, :, :], top_no[:, :, 0:K]))
                s.wait()
                s.did(V.tensor_tensor(onehot[:, :, :],
                                      expert_no[:, :].rearrange("p (a e) -> p a e", a=1).to_broadcast((P, TPG * K, E)),
                                      chosen[:, :, :].rearrange("p a b -> p (a b)").rearrange("p (a b) -> p a b", b=1).to_broadcast((P, TPG * K, E)),
                                      ALU.is_equal))
                s.wait()
                oh = onehot[:, :, :].rearrange("p (a k) e -> p a k e", k=K)
                V.tensor_tensor(member[:, :, :], oh[:, :, 0, :], oh[:, :, 1, :], ALU.add).then_inc(s_member, 1)
                s.end()

            def slot(g, b, before):
                s = Steps(dve, s_slots, g, SLOT_STEPS)
                dve.wait_ge(s_rank, g + 1)
                s.did(V.tensor_tensor(place[:, :, :], bank[7][:, E:(TPG + 1) * E].rearrange("p (a e) -> p a e", a=TPG),
                                      base[:, :].rearrange("p (a e) -> p a e", a=1).to_broadcast((P, TPG, E)), ALU.add))
                dve.wait_ge(s_gexp, g + 1)
                V.tensor_scalar(gate_sum[:, :], gate_exp[:, :], 1.0 / K, 1.0 / K, ALU.mult, ALU.add)
                bin_wait(dve, b, before)
                for j in range(K):
                    V.tensor_scalar(row_out[:, b, j, :, D:D + 1].rearrange("p a b -> p (a b)"), tiles_of(token2, g),
                                    float(j), None, ALU.add)
                s.wait()
                for j in range(K):
                    V.tensor_tensor(picked[:, :, :].rearrange("p (a k) e -> p a k e", k=K)[:, :, j, :],
                                          onehot[:, :, :].rearrange("p (a k) e -> p a k e", k=K)[:, :, j, :],
                                          place[:, :, :], ALU.mult)
                s.did(V.tensor_tensor(base[:, :], base[:, :], bank[7][:, (TPG + 1) * E:(TPG + 2) * E], ALU.add))
                s.wait()
                s.did(V.reciprocal(row_out[:, b, 0, :, D + 1:D + 2].rearrange("p a b -> p (a b)"), gate_sum[:, :]))
                s.wait()
                V.tensor_tensor(row_out[:, b, 1, :, D + 1:D + 2].rearrange("p a b -> p (a b)"), gate_exp[:, :],
                                row_out[:, b, 0, :, D + 1:D + 2].rearrange("p a b -> p (a b)"), ALU.mult)
                with nc.allow_low_precision(reason="summed in float32; row numbers are whole"):
                    V.tensor_reduce(slots[:, b, :, :].rearrange("p a k -> p (a k)"), picked[:, :, :], AX_X,
                                    ALU.add).then_inc(s_slot, 1)
                s.end()

            dve.wait_ge(s_const, 1)
            turns(dve, body)

            tb = Steps(dve, s_tab, 0, 999)
            dve.wait_ge(s_slots, G * SLOT_STEPS)
            tb.did(V.tensor_copy(base_i[:, :], base[:, :]))
            tb.did(V.tensor_tensor(cnt[:, :], base[:, :], bin_start[:, :], ALU.subtract))
            tb.wait()
            tb.did(V.tensor_scalar(cnt_i[:, :], cnt[:, :], float(P - 1), None, ALU.add))
            tb.did(V.memset(scan[0][:, :], 0.0))
            tb.did(V.memset(scan[1][:, :], 0.0))
            tb.wait()
            tb.did(V.tensor_scalar(ntile_i[:, :], cnt_i[:, :], 7, None, ALU.logical_shift_right))
            tb.wait()
            tb.did(V.tensor_copy(scan[0][:, PADC:], ntile_i[:, :]))
            for n, by in enumerate((1, 2, 4, 8)):
                tb.wait()
                a, b = scan[n % 2], scan[1 - n % 2]
                tb.did(V.tensor_tensor(b[:, PADC:], a[:, PADC:], a[:, PADC - by:PADC + E - by], ALU.add))
            tb.wait()
            ends = scan[0][:, PADC:].rearrange("p (a e) -> p a e", a=1).to_broadcast((P, XC, E))
            tb.did(V.tensor_tensor(passed[:, :, :], ends,
                                   tile_no[:, :].rearrange("p (a e) -> p a e", e=1).to_broadcast((P, XC, E)), ALU.is_le))
            tb.wait()
            tb.did(V.tensor_reduce(col[:, 0, :], passed[:, :, :], AX_X, ALU.add))
            tb.did(V.tensor_tensor(passed_ends[:, :, :], passed[:, :, :], ends, ALU.mult))
            tb.wait()
            tb.did(V.tensor_reduce(col[:, 1, :], passed_ends[:, :, :], AX_X, ALU.max))
            tb.did(V.tensor_scalar(col[:, 3, :], col[:, 0, :], float(E - 1), None, ALU.min))
            tb.wait()
            tb.did(V.tensor_tensor(col[:, 1, :], tile_no[:, :], col[:, 1, :], ALU.subtract))
            tb.did(V.tensor_scalar(col[:, 2, :], col[:, 0, :], float(BIN), None, ALU.mult))
            tb.wait()
            tb.did(V.scalar_tensor_tensor(out=col[:, 2, :], in0=col[:, 1, :], scalar=float(P), in1=col[:, 2, :],
                                          op0=ALU.mult, op1=ALU.add))
            tb.wait()
            for j in range(2):
                for c in range(XC):
                    last = V.tensor_scalar(diag[0:XP, j, c * XP:(c + 1) * XP], ident[0:XP, 0:XP], col[0:XP, 2 + j, c:c + 1],
                                           None, ALU.mult)
            last.then_inc(s_diag, 1)
            tb.did(V.memset(expert_i[:, 0:BEFORE], 0))
            tb.did(V.memset(expert_i[:, BEFORE + XT:], 0))
            dve.wait_ge(s_spread, 1)
            tb.did(V.tensor_copy(expert_i[:, BEFORE:BEFORE + XT], bank[0][:, XT:2 * XT]))
            V.tensor_scalar(first_row_i[:, :], bank[0][:, 0:XT], float(PAD_ROW), None, ALU.min).then_inc(s_tab_done, 1)

            dve.wait_ge(s_late, 16 * 5)
            dve.wait_ge(s_tab_done, 1)

            def out_of(t, u, e, tn):
                v = u % XS
                dve.wait_ge(s_mm2, t + 1)
                wait_for(dve, s_sc[v], 16 * (tn * XR + u // XS))
                V.tensor_tensor(y[:, v, :], bank[6 + u % 2][:, 0:D], b2_all[:, bass.ds(e * D, D)], ALU.add).then_inc(s_biased, 1)
                V.tensor_copy(dest[:, v:v + 1], xg[:, v, D:D + 1])
                dve.wait_ge(s_biased, t + 1)
                V.scalar_tensor_tensor(out=y[:, v, :], in0=y[:, v, :], scalar=xg[:, v, D + 1:D + 2], in1=xg[:, v, 0:D],
                                       op0=ALU.mult, op1=ALU.add).then_inc(s_y, 1)

            def add_beta(g):
                V.tensor_tensor(xg_of(g), xg_of(g), beta_all[:, :].rearrange("p (a d) -> p a d", a=1).to_broadcast((P, TPG, D)),
                                ALU.add).then_inc(s_beta, 1)

            def ffn(k, first=False, last=False):
                no, regs = int_registers(dve, expert_i, k * TU, BEFORE + TU, E - 1)
                for u in range(TU):
                    t = k * TU + u
                    if u % XS == XS // 2 and not last:
                        add_beta(k * XR + u // XS)
                    if u >= BEFORE:
                        out_of(t - BEFORE, u - BEFORE, no[u], k)
                    elif not first:
                        out_of(t - BEFORE, TU - BEFORE + u, no[u], k - 1)
                if last:
                    for u in range(BEFORE):
                        out_of(TURNS * TU - BEFORE + u, TU - BEFORE + u, no[TU + u], TURNS - 1)
                free_registers(dve, regs)
            ffn(0, first=True)
            with dve.Fori(1, TURNS - 1) as k:
                ffn(k)
            ffn(TURNS - 1, last=True)

            def last_stage(g, b):
                if has(g, 0):
                    dve.wait_ge(s_yy[b], 16 * (g // YB) + 16 if isinstance(g, int) else (g - b) * (16 // YB) + 16)
                    V.tensor_tensor(yy[:, b, :, 0:D], yy[:, b, :, 0:D], yy[:, b, :, D:2 * D], ALU.add).then_inc(s_sum, 1)
                if has(g, YB):
                    dve.wait_ge(s_fg, g - YB + 1)
                    V.tensor_tensor(xg_of(g - YB), outn[:, b, :, :], xg_of(g - YB), ALU.add).then_inc(s_fo, 1)
                if has(g, 1):
                    o = (b + 1) % 2 * TPG
                    dve.wait_ge(s_frs, g)
                    V.scalar_tensor_tensor(out=shift[:, o:o + TPG], in0=mv[:, 0:TPG, 0:1].rearrange("p a b -> p (a b)"),
                                           scalar=-1.0, in1=rstd[:, o:o + TPG], op0=ALU.mult,
                                           op1=ALU.mult).then_inc(s_shift, 1)
                if has(g, 0):
                    dve.wait_ge(s_sum, g + 1)
                    settle(dve)
                    for i in range(TPG):
                        r = V.bn_stats(bn[:, i, :], yy[:, b, i, 0:D])
                    r.then_inc(s_fs, 1)
                    dve.wait_ge(s_fs, g + 1)
                    settle(dve)
                    for i in range(TPG):
                        r = V.bn_aggr(mv[:, i, :], bn[:, i, :])
                    r.then_inc(s_fmv, 1)
            dve.wait_ge(s_beta, G)
            last_turns(dve, last_stage)


_INS = ["x", "adj", "L0_gnn_W", "L0_gnn_a_1", "L0_gnn_a_2", "L0_gnn_a_12", "L0_gnn_W_1", "L0_gnn_W_2", "L0_ffn_gate_w",
        "L0_ffn_gate_b", "L0_ffn_w1", "L0_ffn_b1", "L0_ffn_w2", "L0_ffn_b2", "L0_ffn_gamma", "L0_ffn_beta"]


def kernel(**inputs):
    import numpy as _np
    import concourse.bacc as _bacc
    from concourse import mybir as _mybir
    from concourse.bass_utils import run_bass_kernel_spmd as _run

    nc = _bacc.Bacc("TRN2", target_bir_lowering=False, num_devices=1)
    arrays, args = {}, []
    for name in _INS:
        a = _np.ascontiguousarray(inputs[name])
        arrays[f"in_{name}_dram"] = a
        args.append(nc.dram_tensor(f"in_{name}_dram", a.shape, _mybir.dt.from_np(a.dtype), kind="ExternalInput").ap())
    out = nc.dram_tensor("out_0_dram", arrays["in_x_dram"].shape, _mybir.dt.float32, kind="ExternalOutput").ap()
    graph_attention_and_routed_experts(nc, *args, out)
    r = _run(nc, [arrays], core_ids=[0])
    return r.results[0]["out_0_dram"]
```
